# Optimizing a Trainium2 kernel written in Bass

```python
import numpy as np
import jax
import jax.numpy as jnp

def _softmax(x, axis=-1):
    return jax.nn.softmax(x, axis=axis)

def _gelu(x):
    return jax.nn.gelu(x, approximate=True)

def _silu(x):
    return jax.nn.silu(x)

def _sigmoid(x):
    return jax.nn.sigmoid(x)

def _layernorm(x, axis=-1, eps=1e-05):
    m = jnp.mean(x, axis=axis, keepdims=True)
    v = jnp.var(x, axis=axis, keepdims=True)
    return (x - m) / jnp.sqrt(v + eps)

def _scatter_add(tgt, idx, src, axis=0):
    return tgt.at[idx].add(src)

def _segment_sum(src, seg, n):
    return jax.ops.segment_sum(src, seg, n)
kernel_name = 'mk_adaln_d1_jaxref_r8_92ca05'

def setup_inputs(seed: int=0):
    np.random.seed(seed)
    _w = jnp.asarray

    def _L0_attn_setup():
        import jax, jax.numpy as jnp
        import numpy as np
        D_MODEL = 128
        NUM_HEADS = 16
        HEAD_DIM = D_MODEL // NUM_HEADS
        key = jax.random.key(seed)
        ks = jax.random.split(key, 5)
        B, S = (1, 512)
        scale = 0.02
        return {'x': jax.random.normal(ks[0], (B, S, D_MODEL), dtype=jnp.float32), 'w_q': jax.random.normal(ks[1], (D_MODEL, D_MODEL), dtype=jnp.float32) * scale, 'w_k': jax.random.normal(ks[2], (D_MODEL, D_MODEL), dtype=jnp.float32) * scale, 'w_v': jax.random.normal(ks[3], (D_MODEL, D_MODEL), dtype=jnp.float32) * scale, 'w_o': jax.random.normal(ks[4], (D_MODEL, D_MODEL), dtype=jnp.float32) * scale}
    _L0_attn_in = _L0_attn_setup()

    def _L0_ffn_setup():
        import jax, jax.numpy as jnp
        import numpy as np
        SL, BS, HS, FF, E, TOPK = (256, 2, 128, 512, 8, 2)
        key = jax.random.key(seed)
        ks = jax.random.split(key, 6)
        T = SL * BS
        x = jax.random.normal(ks[0], (SL, BS, HS), jnp.float32)
        scores = jax.random.uniform(ks[1], (T, E), jnp.float32)
        expert_weights = jax.random.uniform(ks[2], (T, TOPK), jnp.float32)
        expert_indices = jax.random.randint(ks[3], (T, TOPK), 0, E, jnp.int32)
        w1 = jax.random.normal(ks[4], (E, HS, FF), jnp.float32) * (1.0 / np.sqrt(HS))
        w2 = jax.random.normal(ks[5], (E, FF, HS), jnp.float32) * (1.0 / np.sqrt(FF))
        bias = jnp.zeros((HS,), jnp.float32)
        return dict(x=x, scores=scores, expert_weights=expert_weights, expert_indices=expert_indices, w1=w1, w2=w2, bias=bias)
    _L0_ffn_in = _L0_ffn_setup()
    _L0_c = _w((lambda *s: np.random.randn(*s).astype(np.float32) * 0.05)(2, 128))
    _L0_wmod = _w((lambda *s: np.random.randn(*s).astype(np.float32) * 0.05)(128, 6 * 128) * 128 ** (-0.5))
    _d = {'L0_attn_x': _L0_attn_in['x'], 'L0_attn_w_q': _L0_attn_in['w_q'], 'L0_attn_w_k': _L0_attn_in['w_k'], 'L0_attn_w_v': _L0_attn_in['w_v'], 'L0_attn_w_o': _L0_attn_in['w_o'], 'L0_ffn_scores': _L0_ffn_in['scores'], 'L0_ffn_expert_weights': _L0_ffn_in['expert_weights'], 'L0_ffn_expert_indices': _L0_ffn_in['expert_indices'], 'L0_ffn_w1': _L0_ffn_in['w1'], 'L0_ffn_w2': _L0_ffn_in['w2'], 'L0_ffn_bias': _L0_ffn_in['bias'], 'L0_c': _L0_c, 'L0_wmod': _L0_wmod}
    _x0 = _d['L0_attn_x']
    _d['L0_attn_x'] = jax.random.normal(jax.random.fold_in(jax.random.key(seed), 1), (2, 1024, 128), dtype=_x0.dtype)
    del _x0
    return _d

def reference(L0_attn_x, L0_attn_w_q, L0_attn_w_k, L0_attn_w_v, L0_attn_w_o, L0_ffn_scores, L0_ffn_expert_weights, L0_ffn_expert_indices, L0_ffn_w1, L0_ffn_w2, L0_ffn_bias, L0_c, L0_wmod):

    def _L0_attn_ref(x, w_q, w_k, w_v, w_o):
        import jax, jax.numpy as jnp
        import numpy as np
        D_MODEL = 128
        NUM_HEADS = 16
        HEAD_DIM = D_MODEL // NUM_HEADS
        B, S, _ = x.shape
        q = x @ w_q.T
        k = x @ w_k.T
        v = x @ w_v.T
        q = q.reshape(B, S, NUM_HEADS, HEAD_DIM)
        k = k.reshape(B, S, NUM_HEADS, HEAD_DIM)
        v = v.reshape(B, S, NUM_HEADS, HEAD_DIM)
        scale = HEAD_DIM ** (-0.5)
        scores = jnp.einsum('bqhd,bkhd->bhqk', q, k) * scale
        weights = jax.nn.softmax(scores, axis=-1)
        out = jnp.einsum('bhqk,bkhd->bqhd', weights, v)
        concat = out.reshape(B, S, D_MODEL)
        return concat @ w_o.T

    def _L0_ffn_ref(x, scores, expert_weights, expert_indices, w1, w2, bias):
        import jax, jax.numpy as jnp
        import numpy as np
        SL, BS, HS, FF, E, TOPK = (256, 2, 128, 512, 8, 2)
        sl, bs, hs = x.shape
        n_exp = w1.shape[0]
        top_k = expert_indices.shape[-1]
        xf = x.reshape(-1, hs)
        flat_idx = expert_indices.reshape(-1)
        flat_w = expert_weights.reshape(-1)
        order = jnp.argsort(flat_idx)
        tok = order // top_k
        tokens_per_expert = jnp.bincount(flat_idx, length=n_exp).astype(jnp.int32)
        xs = xf[tok]
        h = jax.nn.gelu(jax.lax.ragged_dot(xs, w1, tokens_per_expert), approximate=False)
        ys = jax.lax.ragged_dot(h, w2, tokens_per_expert)
        ys = ys * flat_w[order][:, None]
        out = jnp.zeros_like(xf).at[tok].add(ys)
        return out.reshape(sl, bs, hs) + bias
    x = L0_attn_x
    mod = (_silu(L0_c) @ L0_wmod).reshape(L0_c.shape[0], 6, 1, -1)
    sa, ca, ga, sb, cb, gb = (mod[:, 0], mod[:, 1], mod[:, 2], mod[:, 3], mod[:, 4], mod[:, 5])
    ga = (2 * (ga >= 0) - 1) * jnp.maximum(jnp.abs(ga), 0.25)
    gb = (2 * (gb >= 0) - 1) * jnp.maximum(jnp.abs(gb), 0.25)
    h = _layernorm(x, axis=-1) * (1 + ca) + sa
    x = x + ga * _L0_attn_ref(h, L0_attn_w_q, L0_attn_w_k, L0_attn_w_v, L0_attn_w_o)
    h = _layernorm(x, axis=-1) * (1 + cb) + sb
    x = x + gb * _L0_ffn_ref(h, L0_ffn_scores, L0_ffn_expert_weights, L0_ffn_expert_indices, L0_ffn_w1, L0_ffn_w2, L0_ffn_bias)
    return x

_drawn_inputs = setup_inputs


def setup_inputs(seed=0):
    import zlib

    import numpy as np

    out = dict(_drawn_inputs(seed))
    spreads = {'L0_ffn_bias': (0.0, 0.317)}
    factors = {'L0_attn_w_q': 8.0, 'L0_attn_w_k': 8.0, 'L0_attn_w_v': 8.0, 'L0_attn_w_o': 8.0}
    for name, (base, spread) in spreads.items():
        noise = np.random.default_rng([zlib.crc32(name.encode()), seed]).standard_normal(out[name].shape)
        drawn = base * np.exp(spread * noise) if base else spread * noise
        out[name] = jnp.asarray(drawn.astype(out[name].dtype))
    for name, factor in factors.items():
        out[name] = (out[name] * factor).astype(out[name].dtype)
    return out
```

```python
from contextlib import ExitStack

import concourse.bass as bass
from concourse import mybir

F32 = mybir.dt.float32
BF16 = mybir.dt.bfloat16
I32 = mybir.dt.int32
ALU = mybir.AluOpType
ACT = mybir.ActivationFunctionType
AX = mybir.AxisListType

P = 128
EPS = 1e-5


def adaln_block(nc, x, w_q, w_k, w_v, w_o, expert_weights, expert_indices, w1, w2, bias, c, wmod, out):
    B, S, D = x.shape
    H, HD = 16, 8
    assert D == P and H * HD == D
    T = B * S
    NT = T // P
    TB = S // P
    CH = 512
    NCH = T // CH
    CT = CH // P
    E, _, FF = w1.shape
    FT, TOPK = expert_indices.shape
    assert FT == CH
    FB = FF // P
    PARTS = 3
    TERMS = 6
    ROWS = TERMS * HD
    MROWS = 2
    HG = 64
    QH = 4
    G = B * H // QH
    HALVES = S // CH
    U = G * HALVES
    SLOTS = 4
    KT = S // P
    VC = HD + 1
    SCALE = float(HD) ** -0.5
    XB = KT * QH
    MT = QH * CT
    PRING = 4

    ctx = ExitStack()
    with ctx:
        def sb(name, shape, dt=F32):
            return ctx.enter_context(nc.sbuf_tensor(name, shape, dt))

        def sem(name):
            return ctx.enter_context(nc.semaphore(name))

        q_rows = nc.dram_tensor("q_rows", [B * H, ROWS, S], BF16).ap()
        k_rows = nc.dram_tensor("k_rows", [B * H, ROWS, S], BF16).ap()
        gate_rows = nc.dram_tensor("gate_rows", [E, FT], F32).ap()

        x_sb = sb("x_sb", [P, NT, D])
        xn = sb("xn", [P, NT, D])
        h_t = sb("h_t", [P, T])
        w_nat = sb("w_nat", [P, 4, D])
        w_t = sb("w_t", [P, 3, D])
        wo_g = sb("wo_g", [P, B, D])
        wo_t = sb("wo_t", [P, B, D])
        wmod_sb = sb("wmod_sb", [P, 6 * D])
        c_sb = sb("c_sb", [B, D])
        c_t = sb("c_t", [P, 5, B])
        mod = sb("mod", [P, 6, B])
        sgn = sb("sgn", [P, 2, B])
        mag = sb("mag", [P, 2, B])
        bias_sb = sb("bias_sb", [P, 1])
        gbb = sb("gbb", [P, B])
        gbb_w = sb("gbb_w", [P, B, P])
        gbb_tok = sb("gbb_tok", [P, B, D])
        ident = sb("ident", [P, P])
        ident_b = sb("ident_b", [P, P], BF16)
        ones = sb("ones", [P, P])
        bn = sb("bn", [P, NT, 6])
        mv = sb("mv", [P, NT, 2])
        ve = sb("ve", [P, NT])
        sd = sb("sd", [P, NT])
        rs = sb("rs", [P, 4, NT])
        split = sb("split", [P, NCH, 2, PARTS, CH], BF16)
        resid = sb("resid", [P, 2, CH])
        v_all = sb("v_all", [P, G, KT, QH, VC])
        v_st = sb("v_st", [P, 2, KT, QH, VC])
        q_buf = [sb(f"q_buf{n}", [P, 2, CH], BF16) for n in range(SLOTS)]
        k_buf = [sb(f"k_buf{n}", [P, 2, S], BF16) for n in range(2)]
        negmax = sb("negmax", [P, 2, CT, 2])
        zeros = sb("zeros", [P, CT, 2])
        mparts = sb("mparts", [P, 2, CT, 2, MROWS], BF16)
        mrow_sb = [sb(f"mrow_sb{n}", [2 * MROWS, CH], BF16) for n in range(2)]
        probs = sb("probs", [P, PRING, QH, CH])
        o_sb = sb("o_sb", [P, CH])
        o_rec = sb("o_rec", [P, CT, QH])
        heads = sb("heads", [P, B, HALVES, CT, D])
        heads_t = sb("heads_t", [P, NCH, CH])
        idx_i = sb("idx_i", [P, CT, TOPK], I32)
        idx_f = sb("idx_f", [P, CT, TOPK])
        ew = sb("ew", [P, CT, TOPK])
        hit = sb("hit", [P, E, CT, TOPK])
        gate = sb("gate", [P, CT, E])
        gate_t = sb("gate_t", [E, FT])
        gate_b = sb("gate_b", [P, E, FT])
        h2_t = sb("h2_t", [P, FT])
        w1_sb = [sb(f"w1_sb{n}", [P, FF]) for n in range(2)]
        w2_sb = [sb(f"w2_sb{n}", [P, FB, D]) for n in range(2)]
        act = sb("act", [P, 2, FT])
        acg = sb("acg", [P, 2, FT])
        y_t = sb("y_t", [P, FT])
        res = sb("res", [P, NT, D])

        ps = ctx.enter_context(nc.psum_tensor("ps", [P, 8, 512], F32))
        row_scores = [ps[:, 0:2, :], ps[:, 2:4, :]]
        col_scores = [ps[:, 4, :], ps[:, 5, :]]
        acc = ps[:, 6, :]
        misc = ps[:, 7, :]

        names = ["c_in", "wts_in", "wmod_in", "small_in", "ident_made", "fills_made",
                 "w_turned", "w_turned_sb", "silu", "mod_mm", "mod_made", "gates_made", "wo_made", "wo_turned",
                 "wo_turned_sb", "stats", "var_ready", "sd_ready", "rstd", "xn_made", "xn_turned", "h_made",
                 "qk_mm", "v_mm", "part_high", "resid_made", "part_mid", "part_low", "v_made", "q_spilled",
                 "k_spilled", "v_staged", "gate_made", "gate_turned", "gate_t_sb", "gate_spilled", "gate_b_in",
                 "gbb_made", "gbb_mm", "gbb_tok_made", "x_biased",
                 "row_mm", "max_done", "max_split", "m_turned", "m_copied", "m_rows_a", "m_rows_b",
                 "col_mm", "exp_done", "value_mm", "acc_copied", "o_turned", "o_rec_made", "o_made",
                 "hd_turned", "hd_sb", "proj_mm", "x1_made", "st2", "var2", "sd2", "rstd2", "xn2", "xn2_turned", "h2_made",
                 "w1_in0", "w1_in1", "w2_in0", "w2_in1", "ff1_mm", "gelu_done", "gated", "ff2_mm", "y_sb", "y_turned",
                 "y_added", "stored"]
        s = {n: sem(n) for n in names}
        x_in = [sem(f"x_in{n}") for n in range(NCH)]
        q_in = [sem(f"q_in{n}") for n in range(SLOTS)]
        v_in = [sem(f"v_in{n}") for n in range(2)]
        k_in = [sem(f"k_in{n}") for n in range(2)]

        block = ctx.enter_context(nc.Block())

        x_rows = x.rearrange("b (t p) d -> p (b t) d", p=P)
        out_rows = out.rearrange("b (t p) d -> p (b t) d", p=P)
        q_write = q_rows.rearrange("(b h) (d t) n -> b (h d) t n", b=B, t=TERMS)
        k_write = k_rows.rearrange("(b h) (d t) n -> b (h d) t n", b=B, t=TERMS)

        def load_q(eng, buf, g, half):
            for par in range(2):
                src = q_rows.rearrange("(g r two) w n -> g two w r n", r=2, two=2)[g, par][:, :, half * CH:(half + 1) * CH]
                eng.dma_start(q_buf[buf][HG * par:HG * par + ROWS, :, :], src).then_inc(q_in[buf], 16)

        def load_k(eng, buf, g):
            for par in range(2):
                src = k_rows.rearrange("(g r two) w n -> g two w r n", r=2, two=2)[g, par]
                eng.dma_start(k_buf[buf][HG * par:HG * par + ROWS, :, :], src).then_inc(k_in[buf], 16)

        def stage_values(eng, buf, g):
            eng.dma_start(v_st[:, buf, :, :, :], v_all[:, g, :, :, :]).then_inc(v_in[buf], 16)

        def send_max_rows(eng, v_next, buf, pair):
            eng.wait_ge(s["m_copied"], 2 * v_next - 1 + pair)
            for par in range(2):
                eng.dma_start(q_buf[buf][HG * par + ROWS:HG * par + ROWS + MROWS, pair, :],
                              mrow_sb[pair][MROWS * par:MROWS * par + MROWS, :]).then_inc(
                                  s["m_rows_b" if pair else "m_rows_a"], 16)

        @block.sync
        def _(sp):
            for n in range(NCH):
                sp.dma_start(x_sb[:, n * CT:(n + 1) * CT, :], x_rows[:, n * CT:(n + 1) * CT, :]).then_inc(x_in[n], 16)
                if n == 0:
                    sp.dma_start(wmod_sb[:, :], wmod).then_inc(s["wmod_in"], 16)
            ew_v = expert_weights.rearrange("(t p) k -> p t k", p=P)
            ei_v = expert_indices.rearrange("(t p) k -> p t k", p=P)
            sp.dma_start(ew[:, :, :], ew_v).then_inc(s["small_in"], 16)
            sp.dma_start(idx_i[:, :, :], ei_v).then_inc(s["small_in"], 16)
            for n in range(NCH):
                b, at = n // HALVES, (n % HALVES) * CH
                sp.wait_ge(s["part_high"], 2 * n + 2)
                sp.wait_ge(s["part_mid"], 2 * n + 2)
                sp.wait_ge(s["part_low"], 2 * n + 2)
                t = 0
                for k in (3, 2, 1):
                    sp.dma_start(q_write[b][:, t:t + k, at:at + CH], split[:, n, 0, 0:k, :]).then_inc(s["q_spilled"], 16)
                    t += k
                t = 0
                for part, k in enumerate((3, 2, 1)):
                    sp.dma_start(k_write[b][:, t:t + k, at:at + CH],
                                 split[:, n, 1, part:part + 1, :].to_broadcast([P, k, CH])).then_inc(s["k_spilled"], 16)
                    t += k
            sp.wait_ge(s["q_spilled"], 48 * NCH)
            sp.wait_ge(s["k_spilled"], 48 * NCH)
            sp.wait_ge(s["fills_made"], 6)
            load_k(sp, 0, 0)
            load_q(sp, 0, 0, 0)
            load_q(sp, 1, 0, 1)
            load_k(sp, 1, 1)
            load_q(sp, 2, 1, 0)
            load_q(sp, 3, 1, 1)
            sp.wait_ge(s["v_made"], NT)
            stage_values(sp, 0, 0)
            stage_values(sp, 1, 1)
            sp.wait_ge(s["gate_t_sb"], 1)
            sp.dma_start(gate_rows[:, :], gate_t[:, :]).then_inc(s["gate_spilled"], 16)
            sp.wait_ge(s["gate_spilled"], 16)
            sp.dma_start(gate_b[:, :, :], gate_rows.rearrange("(o e) t -> o e t", o=1).to_broadcast([P, E, FT])).then_inc(s["gate_b_in"], 16)
            send_max_rows(sp, 1, 0, 0)
            send_max_rows(sp, 1, 0, 1)

            def slots(i, last):
                for t in range(SLOTS):
                    u = i * SLOTS + t
                    if not (last and t == SLOTS - 1):
                        send_max_rows(sp, u + 2, (t + 1) % SLOTS, 0)
                        send_max_rows(sp, u + 2, (t + 1) % SLOTS, 1)
                    if not last:
                        sp.wait_ge(s["col_mm"], (u + 1) * XB)
                        load_q(sp, t, i * 2 + t // 2 + 2, t % 2)
                        if t % 2 == 1:
                            load_k(sp, t // 2, i * 2 + t // 2 + 2)
                            sp.wait_ge(s["value_mm"], PRING + KT * (u + 1))
                            stage_values(sp, t // 2, i * 2 + t // 2 + 2)

            with sp.Fori(0, U // SLOTS - 1) as i:
                slots(i, False)
            slots(U // SLOTS - 1, True)

            w1_v = w1.rearrange("e k f -> k e f")
            w2_v = w2.rearrange("e (b p) d -> p e b d", p=P)

            for n in range(2):
                sp.dma_start(w1_sb[n][:, :], w1_v[:, n, :]).then_inc(s[f"w1_in{n}"], 16)
                sp.dma_start(w2_sb[n][:, :, :], w2_v[:, n, :, :]).then_inc(s[f"w2_in{n}"], 16)
            for n in range(1, NCH):
                sp.wait_ge(s["x1_made"], (n + 1) * CT)
                sp.dma_start(out_rows[:, n * CT:(n + 1) * CT, :], res[:, n * CT:(n + 1) * CT, :]).then_inc(s["stored"], 16)
            with sp.Fori(0, E // 2 - 1) as i:
                for n in range(2):
                    sp.wait_ge(s["ff1_mm"], (i * 2 + n + 1) * FB)
                    sp.dma_start(w1_sb[n][:, :], w1_v[:, i * 2 + n + 2, :]).then_inc(s[f"w1_in{n}"], 16)
                    sp.wait_ge(s["ff2_mm"], (i * 2 + n + 1) * FB)
                    sp.dma_start(w2_sb[n][:, :, :], w2_v[:, i * 2 + n + 2, :, :]).then_inc(s[f"w2_in{n}"], 16)
            sp.wait_ge(s["y_added"], CT)
            sp.dma_start(out_rows[:, 0:CT, :], res[:, 0:CT, :]).then_inc(s["stored"], 16)
            sp.wait_ge(s["stored"], 16 * NCH)

        @block.gpsimd
        def _(pool):
            pool.memset(ident[:, :], 0.0).then_inc(s["fills_made"], 1)
            pool.wait_ge(s["fills_made"], 1)
            pool.affine_select(out=ident[:, :], in_=ident[:, :], compare_op=ALU.not_equal, fill=1.0, base=0,
                               pattern=[[-1, P]], channel_multiplier=1).then_inc(s["ident_made"], 1)
            pool.wait_ge(s["ident_made"], 1)
            pool.tensor_copy(ident_b[:, :], ident[:, :]).then_inc(s["ident_made"], 1)
            pool.memset(ones[:, :], 1.0).then_inc(s["fills_made"], 1)
            pool.memset(v_all[:, :, :, :, :], 1.0).then_inc(s["fills_made"], 1)
            pool.memset(k_buf[0][:, :, :], 1.0).then_inc(s["fills_made"], 1)
            pool.memset(k_buf[1][:, :, :], 1.0).then_inc(s["fills_made"], 1)
            pool.memset(zeros[:, :, :], 0.0).then_inc(s["fills_made"], 1)
            for n in range(2 * NCH):
                pool.wait_ge(s["part_mid"], n + 1)
                pool.tensor_tensor(split[:, n // 2, n % 2, 2, :], resid[:, n % 2, :], split[:, n // 2, n % 2, 1, :],
                                   ALU.subtract).then_inc(s["part_low"], 1)

            pool.wait_ge(s["gbb_tok_made"], 1)
            pool.wait_ge(s["xn_made"], NT)
            for n in range(CT, NT):
                pool.tensor_tensor(x_sb[:, n, :], x_sb[:, n, :], gbb_tok[:, n // TB, :], ALU.add).then_inc(s["x_biased"], 1)

            def split_max(v_next):
                for pair in range(2):
                    pool.wait_ge(s["max_done"], 2 + MT * (v_next - 1) + (pair + 1) * MT // 2)
                    pool.tensor_tensor(mparts[:, pair, :, :, 0], negmax[:, pair, :, :], zeros[:, :, :],
                                       ALU.add).then_inc(s["max_split"], 1)
                    pool.wait_ge(s["max_split"], 4 * v_next - 3 + 2 * pair)
                    pool.tensor_tensor(mparts[:, pair, :, :, 1], negmax[:, pair, :, :], mparts[:, pair, :, :, 0],
                                       ALU.subtract).then_inc(s["max_split"], 1)

            pool.wait_ge(s["fills_made"], 6)
            split_max(1)

            def slots(i, last):
                for t in range(SLOTS):
                    u = i * SLOTS + t
                    if not (last and t == SLOTS - 1):
                        split_max(u + 2)
            with pool.Fori(0, U // SLOTS - 1) as i:
                slots(i, False)
            slots(U // SLOTS - 1, True)

        @block.scalar
        def _(ac):
            ac.dma_start(c_sb[:, :], c).then_inc(s["c_in"], 16)
            for n, w in enumerate((w_q, w_k, w_v, w_o)):
                ac.dma_start(w_nat[:, n, :], w).then_inc(s["wts_in"], 16)
            ac.dma_start(bias_sb[:, :], bias.rearrange("(p o) -> p o", o=1)).then_inc(s["small_in"], 16)
            ac.wait_ge(s["w_turned"], 1)
            ac.activation(c_t[:, 0, :], ps[:, 0, 384:384 + B], ACT.Exp, scale=-1.0).then_inc(s["silu"], 1)
            ac.activation(w_t[:, :, :], ps[:, 0, 0:384].rearrange("p (n d) -> p n d", n=3), ACT.Copy).then_inc(s["w_turned_sb"], 1)
            for b in range(B):
                ac.wait_ge(s["var_ready"], b + 1)
                ac.activation(sd[:, b * TB:(b + 1) * TB], ve[:, b * TB:(b + 1) * TB], ACT.Sqrt).then_inc(s["sd_ready"], 1)
            ac.wait_ge(s["mod_made"], 2)
            for n in range(NCH):
                b = n // HALVES
                ac.wait_ge(s["xn_turned"], n + 1)
                ac.activation(h_t[:, n * CH:(n + 1) * CH], ps[:, 2 + n % 2, :], ACT.Identity,
                              bias=mod[:, 0, b:b + 1], scale=mod[:, 1, b:b + 1]).then_inc(s["h_made"], 1)
                for w in range(2):
                    ac.wait_ge(s["qk_mm"], 2 * n + w + 1)
                    ac.activation(split[:, n, w, 0, :], ps[:, 4 + w, :], ACT.Copy).then_inc(s["part_high"], 1)
                ac.wait_ge(s["fills_made"], 3)
                ac.wait_ge(s["v_mm"], n + 1)
                for t in range(CT):
                    tile = n * CT + t
                    ac.activation(v_all[:, (tile // TB) * (G // B):(tile // TB + 1) * (G // B), tile % TB, :, 0:HD],
                                  ps[:, 6, t * P:(t + 1) * P].rearrange("p (q j d) -> p q j d", q=G // B, j=QH),
                                  ACT.Copy).then_inc(s["v_made"], 1)
                for w in range(2):
                    ac.wait_ge(s["resid_made"], 2 * n + w + 1)
                    ac.activation(split[:, n, w, 1, :], resid[:, w, :], ACT.Copy).then_inc(s["part_mid"], 1)
            ac.wait_ge(s["gbb_made"], B + 1)
            ac.wait_ge(s["gbb_mm"], B)
            ac.activation(gbb_tok[:, :, :], ps[:, 1, 0:B * D].rearrange("p (b d) -> p b d", b=B), ACT.Copy).then_inc(s["gbb_tok_made"], 1)
            ac.wait_ge(s["wo_turned"], 1)
            ac.activation(wo_t[:, :, :], ps[:, 7, 0:B * D].rearrange("p (b d) -> p b d", b=B), ACT.Copy).then_inc(s["exp_done"], 2)

            def copy_max(pair, v_next):
                ac.wait_ge(s["m_turned"], 2 * v_next - 1 + pair)
                ac.activation(mrow_sb[pair][:, :], misc_b[0:2 * MROWS, :], ACT.Copy).then_inc(s["m_copied"], 1)

            def copy_acc(u_next):
                ac.wait_ge(s["value_mm"], PRING + KT * u_next)
                ac.activation(o_sb[:, :], acc, ACT.Copy).then_inc(s["acc_copied"], 1)

            misc_b = misc.bitcast(BF16)[:, 0:CH]
            copy_max(0, 1)
            copy_max(1, 1)

            def slots(i, last):
                for t in range(SLOTS):
                    u = i * SLOTS + t
                    for n in range(XB):
                        kt, j = n // QH, n % QH
                        if j == 0:
                            ac.wait_ge(s["value_mm"], KT * u + kt + 1)
                        ac.wait_ge(s["col_mm"], XB * u + n + 1)
                        ac.activation(probs[:, kt % PRING, j, :], col_scores[n % 2], ACT.Exp,
                                      scale=SCALE).then_inc(s["exp_done"], 1)
                        if n == ACC_AFTER and t > 0:
                            copy_acc(u)
                        if not (last and t == SLOTS - 1):
                            if n == MA_AFTER + 1:
                                copy_max(0, u + 2)
                            if n == MB_AFTER + 1:
                                copy_max(1, u + 2)
                copy_acc((i + 1) * SLOTS)

            with ac.Fori(0, U // SLOTS - 1) as i:
                slots(i, False)
            slots(U // SLOTS - 1, True)

            for n in range(NCH):
                ac.wait_ge(s["hd_turned"], n + 1)
                ac.activation(heads_t[:, n, :], ps[:, 4 + n % 2, :], ACT.Copy).then_inc(s["hd_sb"], 1)
            ac.wait_ge(s["var2"], 1)
            ac.activation(sd[:, 0:CT], ve[:, 0:CT], ACT.Sqrt).then_inc(s["sd2"], 1)
            ac.wait_ge(s["xn2_turned"], 1)
            ac.activation(h2_t[:, :], ps[:, 6, :], ACT.Identity, bias=mod[:, 3, 0:1], scale=mod[:, 4, 0:1]).then_inc(s["h2_made"], 1)

            def gelus(i):
                for n in range(2 * FB):
                    g = i * 2 * FB + n
                    ac.wait_ge(s["ff1_mm"], g + 1)
                    ac.wait_ge(s["gated"], g + 1)
                    ac.activation(act[:, n % 2, :], ps[:, n % 2, :], ACT.Gelu).then_inc(s["gelu_done"], 1)

            with ac.Fori(0, E // 2) as i:
                gelus(i)
            ac.wait_ge(s["ff2_mm"], E * FB)
            ac.activation(y_t[:, :], ps[:, 2, :], ACT.Identity, bias=gbb[:, 0:1], scale=mod[:, 5, 0:1]).then_inc(s["y_sb"], 1)

        @block.vector
        def _(ve_):
            v = ve_

            def rstd_chain(a, b, ready_sem, ready, count, chain_sem):
                v.wait_ge(ready_sem, ready)
                v.reciprocal(rs[:, 0, a:b], sd[:, a:b]).then_inc(chain_sem, 1)
                v.wait_ge(chain_sem, count + 1)
                v.tensor_tensor(rs[:, 1, a:b], rs[:, 0, a:b], rs[:, 0, a:b], ALU.mult).then_inc(chain_sem, 1)
                v.wait_ge(chain_sem, count + 2)
                v.tensor_tensor(rs[:, 2, a:b], rs[:, 1, a:b], ve[:, a:b], ALU.mult).then_inc(chain_sem, 1)
                v.wait_ge(chain_sem, count + 3)
                v.tensor_scalar(rs[:, 1, a:b], rs[:, 2, a:b], -0.5, 1.5, ALU.mult, ALU.add).then_inc(chain_sem, 1)
                v.wait_ge(chain_sem, count + 4)
                v.tensor_tensor(rs[:, 3, a:b], rs[:, 0, a:b], rs[:, 1, a:b], ALU.mult).then_inc(chain_sem, 1)
                v.wait_ge(chain_sem, count + 5)

            v.wait_ge(s["silu"], 1)
            v.tensor_scalar(c_t[:, 1, :], c_t[:, 0, :], 1.0, None, ALU.add).then_inc(s["silu"], 1)
            v.wait_ge(s["silu"], 2)
            v.reciprocal(c_t[:, 2, :], c_t[:, 1, :]).then_inc(s["silu"], 1)
            v.wait_ge(s["silu"], 3)
            v.wait_ge(s["w_turned_sb"], 1)
            v.tensor_tensor(c_t[:, 3, :], ps[:, 0, 384:384 + B], c_t[:, 2, :], ALU.mult).then_inc(s["silu"], 1)
            v.wait_ge(s["mod_mm"], 1)
            v.tensor_copy(mod[:, :, :], ps[:, 1, 0:6 * B].rearrange("p (n b) -> p n b", n=6)).then_inc(s["mod_made"], 1)
            v.wait_ge(s["mod_made"], 1)
            v.tensor_scalar(mod[:, 1:5:3, :], mod[:, 1:5:3, :], 1.0, None, ALU.add).then_inc(s["mod_made"], 1)
            done = 0
            for b in range(B):
                for t in range(TB):
                    n = b * TB + t
                    if t % CT == 0:
                        v.wait_ge(x_in[n // CT], 16)
                    v.bn_stats(bn[:, n, :], x_sb[:, n, :]).then_inc(s["stats"], 1)
                    done += 1
                for t in range(TB):
                    n = b * TB + t
                    v.wait_ge(s["stats"], done - TB + t + 1)
                    v.bn_aggr(mv[:, n, :], bn[:, n, :]).then_inc(s["stats"], 1)
                done += TB
                v.wait_ge(s["stats"], done)
                v.tensor_scalar(ve[:, b * TB:(b + 1) * TB], mv[:, b * TB:(b + 1) * TB, 1], EPS, None, ALU.add).then_inc(s["var_ready"], 1)
                rstd_chain(b * TB, (b + 1) * TB, s["sd_ready"], b + 1, 5 * b, s["rstd"])
                for t in range(TB):
                    n = b * TB + t
                    v.tensor_scalar(xn[:, n, :], x_sb[:, n, :], mv[:, n, 0:1], rs[:, 3, n:n + 1],
                                    ALU.subtract, ALU.mult).then_inc(s["xn_made"], 1)
            v.tensor_scalar(sgn[:, :, :], mod[:, 2:6:3, :], 0.0, 2.0, ALU.is_ge, ALU.mult).then_inc(s["gates_made"], 1)
            v.scalar_tensor_tensor(out=mag[:, :, :], in0=mod[:, 2:6:3, :], scalar=-1.0, in1=mod[:, 2:6:3, :],
                                   op0=ALU.mult, op1=ALU.max).then_inc(s["gates_made"], 1)
            v.wait_ge(s["gates_made"], 2)
            v.tensor_scalar(mag[:, :, :], mag[:, :, :], 0.25, None, ALU.max).then_inc(s["gates_made"], 1)
            v.wait_ge(s["gates_made"], 3)
            v.scalar_tensor_tensor(out=mod[:, 2:6:3, :], in0=sgn[:, :, :], scalar=-1.0, in1=mag[:, :, :],
                                   op0=ALU.add, op1=ALU.mult).then_inc(s["gates_made"], 1)
            v.wait_ge(s["gates_made"], 4)
            v.wait_ge(s["wts_in"], 64)
            for b in range(B):
                v.tensor_scalar(wo_g[:, b, :], w_nat[:, 3, :], mod[:, 2, b:b + 1], None, ALU.mult).then_inc(s["wo_made"], 1)
            v.wait_ge(s["small_in"], 48)
            v.tensor_scalar(gbb[:, :], mod[:, 5, :], bias_sb[:, 0:1], None, ALU.mult).then_inc(s["gbb_made"], 1)
            v.wait_ge(s["gbb_made"], 1)
            v.wait_ge(s["fills_made"], 2)
            for b in range(B):
                v.tensor_scalar(gbb_w[:, b, :], ones[:, :], gbb[:, b:b + 1], None, ALU.mult).then_inc(s["gbb_made"], 1)
            for n in range(2 * NCH):
                v.wait_ge(s["part_high"], n + 1)
                if n >= 2:
                    v.wait_ge(s["part_low"], n - 1)
                v.tensor_tensor(resid[:, n % 2, :], ps[:, 4 + n % 2, :], split[:, n // 2, n % 2, 0, :],
                                ALU.subtract).then_inc(s["resid_made"], 1)
            v.tensor_copy(idx_f[:, :, :], idx_i[:, :, :]).then_inc(s["gate_made"], 1)
            v.wait_ge(s["gate_made"], 1)
            for e in range(E):
                v.scalar_tensor_tensor(out=hit[:, e, :, :], in0=idx_f[:, :, :], scalar=float(e), in1=ew[:, :, :],
                                       op0=ALU.is_equal, op1=ALU.mult).then_inc(s["gate_made"], 1)
            v.wait_ge(s["gate_made"], 1 + E)
            v.tensor_reduce(gate[:, :, :].rearrange("p t e -> p e t"), hit[:, :, :, :], AX.X, ALU.add).then_inc(s["gate_made"], 1)
            v.wait_ge(s["gate_turned"], 1)
            v.tensor_copy(gate_t[:, :], ps[0:E, 0, :]).then_inc(s["gate_t_sb"], 1)
            v.wait_ge(s["v_made"], NT)
            v.memset(acc, 0.0).then_inc(s["value_mm"], PRING)
            v.wait_ge(s["gate_t_sb"], 1)
            v.tensor_copy(o_rec[:, 0, 0:1], ones[:, 0:1]).then_inc(s["max_done"], 2)

            def row_max(v_next, m):
                v.wait_ge(s["row_mm"], MT * (v_next - 1) + m + 1)
                j, t = m // CT, m % CT
                v.tensor_reduce(negmax[:, j // 2, t, j % 2:j % 2 + 1], row_scores[m % 2].rearrange("p a k -> p (a k)"),
                                AX.X, ALU.max, negate=True).then_inc(s["max_done"], 1)

            def normalise(u_next, b, quad, half):
                o = misc.rearrange("p (t j w) -> p t j w", t=CT, j=QH)
                v.wait_ge(s["o_turned"], u_next)
                v.reciprocal(o_rec[:, :, :], o[:, :, :, HD]).then_inc(s["o_rec_made"], 1)
                v.wait_ge(s["o_rec_made"], u_next)
                v.tensor_tensor(heads[:, b, half, :, bass.ds(quad * QH * HD, QH * HD)].rearrange("p t (j d) -> p t j d", j=QH), o[:, :, :, 0:HD],
                                o_rec[:, :, :].rearrange("p t (j o) -> p t j o", o=1).to_broadcast([P, CT, QH, HD]),
                                ALU.mult).then_inc(s["o_made"], 1)

            for m in range(MT):
                row_max(1, m)

            def slots(i, last):
                for t in range(SLOTS):
                    u = i * SLOTS + t
                    for m in range(MT):
                        if not (last and t == SLOTS - 1):
                            row_max(u + 2, m)
                        if m == NORM_AFTER and t > 0:
                            normalise(u, i // 2, i % 2 * 2 + (t - 1) // 2, (t - 1) % 2)
                normalise((i + 1) * SLOTS, i // 2, i % 2 * 2 + 1, 1)

            with v.Fori(0, U // SLOTS - 1) as i:
                slots(i, False)
            slots(U // SLOTS - 1, True)

            for n in range(NCH):
                v.wait_ge(s["proj_mm"], n + 1)
                if n == 1:
                    v.wait_ge(s["x_biased"], NT - CT)
                for t in range(CT):
                    v.tensor_tensor(res[:, n * CT + t, :], ps[:, n % 2, t * P:(t + 1) * P], x_sb[:, n * CT + t, :],
                                    ALU.add).then_inc(s["x1_made"], 1)
                if n == 0:
                    for t in range(CT):
                        v.wait_ge(s["x1_made"], t + 1)
                        v.bn_stats(bn[:, t, :], res[:, t, :]).then_inc(s["st2"], 1)
                    for t in range(CT):
                        v.wait_ge(s["st2"], t + 1)
                        v.bn_aggr(mv[:, t, :], bn[:, t, :]).then_inc(s["st2"], 1)
                    v.wait_ge(s["st2"], 2 * CT)
                    v.tensor_scalar(ve[:, 0:CT], mv[:, 0:CT, 1], EPS, None, ALU.add).then_inc(s["var2"], 1)
                    rstd_chain(0, CT, s["sd2"], 1, 0, s["rstd2"])
                    for t in range(CT):
                        v.tensor_scalar(xn[:, t, :], res[:, t, :], mv[:, t, 0:1], rs[:, 3, t:t + 1],
                                        ALU.subtract, ALU.mult).then_inc(s["xn2"], 1)
            v.wait_ge(s["gate_b_in"], 16)
            v.tensor_copy(o_rec[:, 0, 0:1], ones[:, 0:1]).then_inc(s["gated"], 2)

            def gates(i):
                for n in range(2 * FB):
                    g = i * 2 * FB + n
                    v.wait_ge(s["gelu_done"], g + 1)
                    v.tensor_tensor(acg[:, n % 2, :], act[:, n % 2, :], gate_b[:, i * 2 + n // FB, :], ALU.mult).then_inc(s["gated"], 1)

            with v.Fori(0, E // 2) as i:
                gates(i)
            v.wait_ge(s["y_turned"], 1)
            for t in range(CT):
                v.tensor_tensor(res[:, t, :], ps[:, 3, t * P:(t + 1) * P], res[:, t, :], ALU.add).then_inc(s["y_added"], 1)

        @block.tensor
        def _(pe):
            pe.wait_ge(s["ident_made"], 2)
            pe.wait_ge(s["wts_in"], 64)
            pe.wait_ge(s["c_in"], 16)
            for n in range(3):
                pe.transpose(ps[:, 0, n * P:(n + 1) * P], w_nat[:, n, :], ident[:, :])
            pe.transpose(ps[:, 0, 384:384 + B], c_sb[:, :], ident[0:B, 0:B]).then_inc(s["w_turned"], 1)
            pe.wait_ge(s["silu"], 4)
            pe.wait_ge(s["wmod_in"], 16)
            for n in range(6):
                mm = pe.matmul(ps[:, 1, n * B:(n + 1) * B], wmod_sb[:, n * D:(n + 1) * D], c_t[:, 3, :], start=True, stop=True)
            mm.then_inc(s["mod_mm"], 1)
            pe.wait_ge(s["w_turned_sb"], 1)

            def turn_xn(n):
                for t in range(CT):
                    pe.wait_ge(s["xn_made"], n * CT + t + 1)
                    mm = pe.transpose(ps[:, 2 + n % 2, t * P:(t + 1) * P], xn[:, n * CT + t, :], ident[:, :])
                mm.then_inc(s["xn_turned"], 1)

            turn_xn(0)
            for n in range(NCH):
                if n + 1 < NCH:
                    if n >= 1:
                        pe.wait_ge(s["h_made"], n)
                    turn_xn(n + 1)
                pe.wait_ge(s["h_made"], n + 1)
                for w in range(2):
                    if n >= 1:
                        pe.wait_ge(s["resid_made"], 2 * n - 1 + w)
                    pe.matmul(ps[:, 4 + w, :], w_t[:, w, :], h_t[:, n * CH:(n + 1) * CH], start=True, stop=True).then_inc(s["qk_mm"], 1)
                if n >= 1:
                    pe.wait_ge(s["v_made"], n * CT)
                for t in range(CT):
                    mm = pe.matmul(ps[:, 6, t * P:(t + 1) * P], h_t[:, (n * CT + t) * P:(n * CT + t + 1) * P], w_t[:, 2, :],
                                   start=True, stop=True)
                mm.then_inc(s["v_mm"], 1)
            pe.wait_ge(s["gbb_made"], 1 + B)
            for b in range(B):
                pe.matmul(ps[:, 1, b * D:(b + 1) * D], gbb_w[:, b, :], ident[:, :], start=True, stop=True).then_inc(s["gbb_mm"], 1)
            pe.wait_ge(s["wo_made"], B)
            for b in range(B):
                mm = pe.transpose(ps[:, 7, b * D:(b + 1) * D], wo_g[:, b, :], ident[:, :])
            mm.then_inc(s["wo_turned"], 1)
            pe.wait_ge(s["gate_made"], 2 + E)
            for t in range(CT):
                mm = pe.transpose(ps[0:E, 0, t * P:(t + 1) * P], gate[:, t, :], ident[:, :])
            mm.then_inc(s["gate_turned"], 1)
            pe.wait_ge(s["exp_done"], 2)
            pe.wait_ge(s["h_made"], NCH)
            pe.wait_ge(s["value_mm"], PRING)

            misc_b = misc.bitcast(BF16)[:, 0:CH]

            def row_tile(v_next, buf, kbuf, m, first):
                j, t = m // CT, m % CT
                r = HG * (j % 2)
                if m == 0:
                    pe.wait_ge(*q_ready(v_next, buf))
                    if first is not None:
                        pe.wait_ge(k_in[kbuf], first)
                pe.wait_ge(s["max_done"], MT * (v_next - 1) + m + 1)
                for a in range(S // 512):
                    mm = pe.matmul(row_scores[m % 2][:, a, :], q_buf[buf][r:r + ROWS, j // 2, t * P:(t + 1) * P],
                                   k_buf[kbuf][r:r + ROWS, j // 2, a * 512:(a + 1) * 512], start=True, stop=True)
                mm.then_inc(s["row_mm"], 1)

            def turn_max(v_next, pair):
                pe.wait_ge(s["max_split"], 4 * v_next - 2 + 2 * pair)
                for t in range(CT):
                    mm = pe.transpose(misc_b[0:2 * MROWS, t * P:(t + 1) * P],
                                      mparts[:, pair, t, :, :].rearrange("p j w -> p (j w)"), ident_b[:, :])
                mm.then_inc(s["m_turned"], 1)

            def turn_out(u_next):
                pe.wait_ge(s["acc_copied"], u_next)
                for t in range(CT):
                    mm = pe.transpose(misc[:, t * P:(t + 1) * P], o_sb[:, t * P:(t + 1) * P], ident[:, :])
                mm.then_inc(s["o_turned"], 1)

            def q_ready(v_next, buf):
                return q_in[buf], q_count[0]

            q_count = [32]
            k_first = 32
            for m in range(MT):
                row_tile(1, 0, 0, m, k_first if m == 0 else None)
            turn_max(1, 0)
            pe.wait_ge(s["m_copied"], 1)
            turn_max(1, 1)

            def slots(i, last):
                for t in range(SLOTS):
                    u = i * SLOTS + t
                    more = not (last and t == SLOTS - 1)
                    nb = (t + 1) % SLOTS
                    q_count[0] = 32 * (i + 1) if t < SLOTS - 1 else 32 * (i + 2)
                    new_k = None
                    if nb % 2 == 0:
                        new_k = 32 * (i + 1) if t < SLOTS - 1 else 32 * (i + 2)
                    m = 0
                    for n in range(XB):
                        kt, j = n // QH, n % QH
                        r = HG * (j % 2)
                        if n == 0:
                            pe.wait_ge(s["m_rows_a"], 32 * (u + 1))
                        if n == 2:
                            pe.wait_ge(s["m_rows_b"], 32 * (u + 1))
                        pe.wait_ge(s["exp_done"], XB * u + n + 1)
                        pe.matmul(col_scores[n % 2], k_buf[t // 2][r:r + ROWS + MROWS, j // 2, kt * P:(kt + 1) * P],
                                  q_buf[t][r:r + ROWS + MROWS, j // 2, :], start=True, stop=True).then_inc(s["col_mm"], 1)
                        while more and m < MT and m * ROW_PACE <= n * 10:
                            row_tile(u + 2, nb, nb // 2, m, new_k)
                            m += 1
                        if n % QH == 1 and kt >= 1:
                            value_tile_at(u, t, i, kt - 1)
                        if n == TURN_OUT_AFTER and t > 0:
                            pe.wait_ge(s["m_copied"], 2 * (u + 1))
                            turn_out(u)
                        if more and n == MA_AFTER:
                            if t > 0:
                                pe.wait_ge(s["o_made"], u)
                            turn_max(u + 2, 0)
                        if more and n == MB_AFTER:
                            pe.wait_ge(s["m_copied"], 2 * (u + 1) + 1)
                            turn_max(u + 2, 1)
                    value_tile_at(u, t, i, KT - 1)
                    if t == SLOTS - 1:
                        if more:
                            pe.wait_ge(s["m_copied"], 2 * (u + 2))
                        else:
                            pe.wait_ge(s["o_made"], u)
                        turn_out(u + 1)
                        pe.wait_ge(s["o_made"], u + 1)

            def value_tile_at(u, t, i, kt):
                pe.wait_ge(s["exp_done"], 2 + XB * u + QH * (kt + 1))
                if kt == 0:
                    if t % 2 == 0:
                        pe.wait_ge(v_in[t // 2], 16 * (i + 1))
                    if t > 0:
                        pe.wait_ge(s["acc_copied"], u)
                for j in range(QH):
                    mm = pe.matmul(acc[32 * j:32 * j + VC, :], v_st[:, t // 2, kt, j, :], probs[:, kt % PRING, j, :],
                                   start=(kt == 0), stop=(kt == KT - 1))
                mm.then_inc(s["value_mm"], 1)

            with pe.Fori(0, U // SLOTS - 1) as i:
                slots(i, False)
            slots(U // SLOTS - 1, True)

            def turn_heads(n):
                b, half = n // HALVES, n % HALVES
                if n >= 2:
                    pe.wait_ge(s["hd_sb"], n - 1)
                for t in range(CT):
                    mm = pe.transpose(ps[:, 4 + n % 2, t * P:(t + 1) * P], heads[:, b, half, t, :],
                                      ident[:, :])
                mm.then_inc(s["hd_turned"], 1)

            turn_heads(0)
            for n in range(NCH):
                if n + 1 < NCH:
                    turn_heads(n + 1)
                pe.wait_ge(s["hd_sb"], n + 1)
                if n >= 2:
                    pe.wait_ge(s["x1_made"], (n - 1) * CT)
                for t in range(CT):
                    mm = pe.matmul(ps[:, n % 2, t * P:(t + 1) * P], heads_t[:, n, t * P:(t + 1) * P], wo_t[:, n // HALVES, :],
                                   start=True, stop=True)
                mm.then_inc(s["proj_mm"], 1)
            for t in range(CT):
                pe.wait_ge(s["xn2"], t + 1)
                mm = pe.transpose(ps[:, 6, t * P:(t + 1) * P], xn[:, t, :], ident[:, :])
            mm.then_inc(s["xn2_turned"], 1)
            pe.wait_ge(s["h2_made"], 1)
            pe.wait_ge(s["x1_made"], NT)

            def ff1(i, n, count):
                if n % FB == 0:
                    pe.wait_ge(s[f"w1_in{n // FB}"], 16 * (i + 1))
                pe.matmul(ps[:, n % 2, :], w1_sb[n // FB][:, (n % FB) * P:(n % FB + 1) * P], h2_t[:, :],
                          start=True, stop=True).then_inc(s["ff1_mm"], 1)

            def ff2(i, n, start, stop):
                if n % FB == 0:
                    pe.wait_ge(s[f"w2_in{n // FB}"], 16 * (i + 1))
                pe.wait_ge(s["gated"], i * 2 * FB + n + 3)
                pe.matmul(ps[:, 2, :], w2_sb[n // FB][:, n % FB, :], acg[:, n % 2, :], start=start, stop=stop,
                          skip_group_check=True).then_inc(s["ff2_mm"], 1)

            def experts(i, first, last):
                for n in range(2 * FB):
                    if not (last and n == 2 * FB - 1):
                        if n + 1 < 2 * FB:
                            ff1(i, n + 1, None)
                        else:
                            ff1(i + 1, 0, None)
                    ff2(i, n, first and n == 0, last and n == 2 * FB - 1)

            ff1(0, 0, None)
            experts(0, True, False)
            with pe.Fori(1, E // 2 - 1) as i:
                experts(i, False, False)
            experts(E // 2 - 1, False, True)
            pe.wait_ge(s["y_sb"], 1)
            for t in range(CT):
                mm = pe.transpose(ps[:, 3, t * P:(t + 1) * P], y_t[:, t * P:(t + 1) * P], ident[:, :])
            mm.then_inc(s["y_turned"], 1)


ACC_AFTER = 3
TURN_OUT_AFTER = 8
NORM_AFTER = 6
MA_AFTER = 18
MB_AFTER = 29
ROW_PACE = 16

_INS = ["L0_attn_x", "L0_attn_w_q", "L0_attn_w_k", "L0_attn_w_v", "L0_attn_w_o", "L0_ffn_expert_weights",
        "L0_ffn_expert_indices", "L0_ffn_w1", "L0_ffn_w2", "L0_ffn_bias", "L0_c", "L0_wmod"]


def kernel(**inputs):
    import numpy as _np
    import concourse.bacc as _bacc
    from concourse import mybir as _mybir
    from concourse.bass_utils import run_bass_kernel_spmd as _run

    nc = _bacc.Bacc("TRN2", target_bir_lowering=False, num_devices=1)
    arrays, args = {}, []
    for name in _INS:
        a = _np.ascontiguousarray(inputs[name])
        arrays[f"in_{name}_dram"] = a
        args.append(nc.dram_tensor(f"in_{name}_dram", a.shape, _mybir.dt.from_np(a.dtype), kind="ExternalInput").ap())
    out = nc.dram_tensor("out_dram", inputs["L0_attn_x"].shape, _mybir.dt.float32, kind="ExternalOutput").ap()
    adaln_block(nc, *args, out)
    r = _run(nc, [arrays], core_ids=[0])
    return r.results[0]["out_dram"]
```

```python
from contextlib import ExitStack

import concourse.bass as bass
from concourse import mybir

F32 = mybir.dt.float32
BF16 = mybir.dt.bfloat16
I32 = mybir.dt.int32
ALU = mybir.AluOpType
ACT = mybir.ActivationFunctionType
AX = mybir.AxisListType

P = 128
EPS = 1e-5


def adaln_block(nc, x, w_q, w_k, w_v, w_o, expert_weights, expert_indices, w1, w2, bias, c, wmod, out):
    B, S, D = x.shape
    H, HD = 16, 8
    assert D == P and H * HD == D
    T = B * S
    NT = T // P
    TB = S // P
    CH = 512
    NCH = T // CH
    CT = CH // P
    E, _, FF = w1.shape
    FT, TOPK = expert_indices.shape
    assert FT == CH
    FB = FF // P
    PARTS = 3
    TERMS = 6
    ROWS = TERMS * HD
    MROWS = 2
    HG = 64
    QH = 4
    G = B * H // QH
    HALVES = S // CH
    U = G * HALVES
    SLOTS = 4
    KT = S // P
    VC = HD + 1
    SCALE = float(HD) ** -0.5
    XB = KT * QH
    MT = QH * CT
    PRING = 4

    ctx = ExitStack()
    with ctx:
        def sb(name, shape, dt=F32):
            return ctx.enter_context(nc.sbuf_tensor(name, shape, dt))

        def sem(name):
            return ctx.enter_context(nc.semaphore(name))

        q_rows = nc.dram_tensor("q_rows", [B * H, ROWS, S], BF16).ap()
        k_rows = nc.dram_tensor("k_rows", [B * H, ROWS, S], BF16).ap()
        gate_rows = nc.dram_tensor("gate_rows", [E, FT], F32).ap()

        x_sb = sb("x_sb", [P, NT, D])
        xn = sb("xn", [P, NT, D])
        h_t = sb("h_t", [P, T])
        w_nat = sb("w_nat", [P, 4, D])
        w_t = sb("w_t", [P, 3, D])
        wo_g = sb("wo_g", [P, B, D])
        wo_t = sb("wo_t", [P, B, D])
        wmod_sb = sb("wmod_sb", [P, 6 * D])
        c_sb = sb("c_sb", [B, D])
        c_t = sb("c_t", [P, 5, B])
        mod = sb("mod", [P, 6, B])
        sgn = sb("sgn", [P, 2, B])
        mag = sb("mag", [P, 2, B])
        bias_sb = sb("bias_sb", [P, 1])
        gbb = sb("gbb", [P, B])
        gbb_w = sb("gbb_w", [P, B, P])
        gbb_tok = sb("gbb_tok", [P, B, D])
        ident = sb("ident", [P, P])
        ident_b = sb("ident_b", [P, P], BF16)
        ones = sb("ones", [P, P])
        bn = sb("bn", [P, NT, 6])
        mv = sb("mv", [P, NT, 2])
        ve = sb("ve", [P, NT])
        sd = sb("sd", [P, NT])
        rs = sb("rs", [P, 4, NT])
        split = sb("split", [P, NCH, 2, PARTS, CH], BF16)
        resid = sb("resid", [P, 2, CH])
        v_all = sb("v_all", [P, G, KT, QH, VC])
        v_st = sb("v_st", [P, 2, KT, QH, VC])
        q_buf = [sb(f"q_buf{n}", [P, 2, CH], BF16) for n in range(SLOTS)]
        k_buf = [sb(f"k_buf{n}", [P, QH, S], BF16) for n in range(2)]
        negmax = sb("negmax", [P, 2, CT, 2])
        zero_rows = sb("zero_rows", [MROWS, 2, CH], BF16)
        zeros = sb("zeros", [P, CT, 2])
        mparts = sb("mparts", [P, 2, CT, 2, MROWS], BF16)
        mrow_sb = [sb(f"mrow_sb{n}", [2 * MROWS, CH], BF16) for n in range(2)]
        probs = sb("probs", [P, PRING, QH, CH])
        o_sb = sb("o_sb", [P, CH])
        o_rec = sb("o_rec", [P, CT, QH])
        heads = sb("heads", [P, B, HALVES, CT, D])
        heads_t = sb("heads_t", [P, NCH, CH])
        idx_i = sb("idx_i", [P, CT, TOPK], I32)
        idx_f = sb("idx_f", [P, CT, TOPK])
        ew = sb("ew", [P, CT, TOPK])
        hit = sb("hit", [P, E, CT, TOPK])
        gate = sb("gate", [P, CT, E])
        gate_t = sb("gate_t", [E, FT])
        gate_b = sb("gate_b", [P, E, FT])
        h2_t = sb("h2_t", [P, FT])
        w1_sb = [sb(f"w1_sb{n}", [P, FF]) for n in range(2)]
        w2_sb = [sb(f"w2_sb{n}", [P, FB, D]) for n in range(2)]
        act = sb("act", [P, 2, FT])
        acg = sb("acg", [P, 2, FT])
        y_t = sb("y_t", [P, FT])
        res = sb("res", [P, NT, D])

        ps = ctx.enter_context(nc.psum_tensor("ps", [P, 8, 512], F32))
        row_scores = [ps[:, 0:2, :], ps[:, 2:4, :]]
        col_scores = [ps[:, 4, :], ps[:, 5, :]]
        acc = ps[:, 6, :]
        misc = ps[:, 7, :]

        names = ["c_in", "wts_in", "wmod_in", "small_in", "ident_made", "fills_made", "k_filled",
                 "w_turned", "w_turned_sb", "silu", "mod_mm", "mod_made", "gates_made", "wo_made", "wo_turned",
                 "wo_turned_sb", "stats", "var_ready", "sd_ready", "rstd", "xn_made", "xn_turned", "h_made",
                 "qk_mm", "v_mm", "part_high", "resid_made", "part_mid", "part_low", "v_made", "q_spilled",
                 "k_spilled", "v_staged", "gate_made", "gate_turned", "gate_t_sb", "gate_spilled", "gate_b_in",
                 "gbb_made", "gbb_mm", "gbb_tok_made", "x_biased",
                 "row_mm", "max_done", "max_split", "m_turned", "m_copied", "m_rows_a", "m_rows_b",
                 "col_mm", "exp_done", "value_mm", "acc_copied", "o_turned", "o_rec_made", "o_made",
                 "hd_turned", "hd_sb", "proj_mm", "x1_made", "st2", "var2", "sd2", "rstd2", "xn2", "xn2_turned", "h2_made",
                 "w1_in0", "w1_in1", "w2_in0", "w2_in1", "ff1_mm", "gelu_done", "gated", "ff2_mm", "y_sb", "y_turned",
                 "y_added", "stored"]
        s = {n: sem(n) for n in names}
        x_in = [sem(f"x_in{n}") for n in range(NCH)]
        q_in = [sem(f"q_in{n}") for n in range(SLOTS)]
        v_in = [sem(f"v_in{n}") for n in range(2)]
        k_in = [sem(f"k_in{n}") for n in range(2)]

        block = ctx.enter_context(nc.Block())

        x_rows = x.rearrange("b (t p) d -> p (b t) d", p=P)
        out_rows = out.rearrange("b (t p) d -> p (b t) d", p=P)
        q_write = q_rows.rearrange("(b h) (d t) n -> b (h d) t n", b=B, t=TERMS)
        k_write = k_rows.rearrange("(b h) (d t) n -> b (h d) t n", b=B, t=TERMS)

        STEPS = SLOTS * KT

        def stream(i, q, lead):
            n = q + lead
            unit = i * SLOTS + n // KT
            if n < 0 or (type(unit) is int and unit >= U):
                return None
            return unit, n // KT % SLOTS, n % KT

        def start_of(i, q, lead):
            found = stream(i, q, lead)
            return found if found is not None and found[2] == 0 else None

        def pipeline(eng, step):
            for q in range(-LEAD_ROW, 0):
                step(0, q)
            with eng.Fori(0, U // SLOTS - 1) as i:
                for q in range(STEPS):
                    step(i, q)
            for q in range(STEPS):
                step(U // SLOTS - 1, q)

        def load_q(eng, buf, g, half):
            for par in range(2):
                src = q_rows.rearrange("(g r two) w n -> g two w r n", r=2, two=2)[g, par][:, :, half * CH:(half + 1) * CH]
                eng.dma_start(q_buf[buf][HG * par:HG * par + ROWS, :, :], src).then_inc(q_in[buf], 16)
                eng.dma_start(q_buf[buf][HG * par + ROWS:HG * par + ROWS + MROWS, :, :], zero_rows[:, :, :]).then_inc(q_in[buf], 16)

        def load_k(eng, buf, g):
            for par in range(2):
                src = k_rows.rearrange("(g r two) w n -> g two w r n", r=2, two=2)[g, par]
                eng.dma_start(k_buf[buf][HG * par:HG * par + ROWS, par::2, :], src).then_inc(k_in[buf], 16)

        def stage_values(eng, buf, g):
            eng.dma_start(v_st[:, buf, :, :, :], v_all[:, g, :, :, :]).then_inc(v_in[buf], 16)

        def send_max_rows(eng, v_next, buf, pair):
            eng.wait_ge(s["m_copied"], 2 * v_next - 1 + pair)
            for par in range(2):
                eng.dma_start(q_buf[buf][HG * par + ROWS:HG * par + ROWS + MROWS, pair, :],
                              mrow_sb[pair][MROWS * par:MROWS * par + MROWS, :]).then_inc(
                                  s["m_rows_b" if pair else "m_rows_a"], 16)

        @block.sync
        def _(sp):
            for n in range(NCH):
                sp.dma_start(x_sb[:, n * CT:(n + 1) * CT, :], x_rows[:, n * CT:(n + 1) * CT, :]).then_inc(x_in[n], 16)
                if n == 0:
                    sp.dma_start(wmod_sb[:, :], wmod).then_inc(s["wmod_in"], 16)
            ew_v = expert_weights.rearrange("(t p) k -> p t k", p=P)
            ei_v = expert_indices.rearrange("(t p) k -> p t k", p=P)
            sp.dma_start(ew[:, :, :], ew_v).then_inc(s["small_in"], 16)
            sp.dma_start(idx_i[:, :, :], ei_v).then_inc(s["small_in"], 16)
            for n in range(NCH):
                b, at = n // HALVES, (n % HALVES) * CH
                sp.wait_ge(s["part_high"], 2 * n + 2)
                sp.wait_ge(s["part_mid"], 2 * n + 2)
                sp.wait_ge(s["part_low"], 2 * n + 2)
                t = 0
                for k in (3, 2, 1):
                    sp.dma_start(q_write[b][:, t:t + k, at:at + CH], split[:, n, 0, 0:k, :]).then_inc(s["q_spilled"], 16)
                    t += k
                t = 0
                for part, k in enumerate((3, 2, 1)):
                    sp.dma_start(k_write[b][:, t:t + k, at:at + CH],
                                 split[:, n, 1, part:part + 1, :].to_broadcast([P, k, CH])).then_inc(s["k_spilled"], 16)
                    t += k
            sp.wait_ge(s["q_spilled"], 48 * NCH)
            sp.wait_ge(s["k_spilled"], 48 * NCH)
            sp.wait_ge(s["fills_made"], 5 + SLOTS)
            sp.wait_ge(s["k_filled"], 8)
            load_k(sp, 0, 0)
            load_q(sp, 0, 0, 0)
            load_q(sp, 1, 0, 1)
            load_k(sp, 1, 1)
            load_q(sp, 2, 1, 0)
            load_q(sp, 3, 1, 1)
            sp.wait_ge(s["v_made"], NT)
            stage_values(sp, 0, 0)
            stage_values(sp, 1, 1)
            sp.wait_ge(s["gate_t_sb"], 1)
            sp.dma_start(gate_rows[:, :], gate_t[:, :]).then_inc(s["gate_spilled"], 16)
            sp.wait_ge(s["gate_spilled"], 16)
            sp.dma_start(gate_b[:, :, :], gate_rows.rearrange("(o e) t -> o e t", o=1).to_broadcast([P, E, FT])).then_inc(s["gate_b_in"], 16)

            def step(i, q):
                if start_of(i, q, LEAD_MA):
                    u, t, _ = stream(i, q, LEAD_MA)
                    send_max_rows(sp, u + 1, t, 0)
                if start_of(i, q, LEAD_MB):
                    u, t, _ = stream(i, q, LEAD_MB)
                    send_max_rows(sp, u + 1, t, 1)
                load = start_of(i, q, LEAD_LOAD)
                if load and not (type(load[0]) is int and load[0] < SLOTS):
                    u, t, _ = load
                    g = i * 2 + (q + LEAD_LOAD) // KT // 2
                    sp.wait_ge(s["col_mm"], (u - 3) * XB)
                    load_q(sp, t, g, t % 2)
                    if t % 2 == 0:
                        sp.wait_ge(s["col_mm"], (u - 2) * XB)
                        load_k(sp, t // 2, g)
                load = start_of(i, q, LEAD_LOAD_V)
                if load and load[1] % 2 == 0 and not (type(load[0]) is int and load[0] < SLOTS):
                    u, t, _ = load
                    sp.wait_ge(s["value_mm"], PRING + KT * (u - 2))
                    stage_values(sp, t // 2, i * 2 + (q + LEAD_LOAD_V) // KT // 2)

            pipeline(sp, step)

            w1_v = w1.rearrange("e k f -> k e f")
            w2_v = w2.rearrange("e (b p) d -> p e b d", p=P)

            for n in range(2):
                sp.dma_start(w1_sb[n][:, :], w1_v[:, n, :]).then_inc(s[f"w1_in{n}"], 16)
                sp.dma_start(w2_sb[n][:, :, :], w2_v[:, n, :, :]).then_inc(s[f"w2_in{n}"], 16)
            for n in range(1, NCH):
                sp.wait_ge(s["x1_made"], (n + 1) * CT)
                sp.dma_start(out_rows[:, n * CT:(n + 1) * CT, :], res[:, n * CT:(n + 1) * CT, :]).then_inc(s["stored"], 16)
            with sp.Fori(0, E // 2 - 1) as i:
                for n in range(2):
                    sp.wait_ge(s["ff1_mm"], (i * 2 + n + 1) * FB)
                    sp.dma_start(w1_sb[n][:, :], w1_v[:, i * 2 + n + 2, :]).then_inc(s[f"w1_in{n}"], 16)
                    sp.wait_ge(s["ff2_mm"], (i * 2 + n + 1) * FB)
                    sp.dma_start(w2_sb[n][:, :, :], w2_v[:, i * 2 + n + 2, :, :]).then_inc(s[f"w2_in{n}"], 16)
            sp.wait_ge(s["y_added"], CT)
            sp.dma_start(out_rows[:, 0:CT, :], res[:, 0:CT, :]).then_inc(s["stored"], 16)
            sp.wait_ge(s["stored"], 16 * NCH)

        @block.gpsimd
        def _(pool):
            pool.memset(ident[:, :], 0.0).then_inc(s["fills_made"], 1)
            pool.wait_ge(s["fills_made"], 1)
            pool.affine_select(out=ident[:, :], in_=ident[:, :], compare_op=ALU.not_equal, fill=1.0, base=0,
                               pattern=[[-1, P]], channel_multiplier=1).then_inc(s["ident_made"], 1)
            pool.wait_ge(s["ident_made"], 1)
            pool.tensor_copy(ident_b[:, :], ident[:, :]).then_inc(s["ident_made"], 1)
            pool.memset(ones[:, :], 1.0).then_inc(s["fills_made"], 1)
            pool.memset(v_all[:, :, :, :, :], 1.0).then_inc(s["fills_made"], 1)
            pool.memset(zero_rows[:, :, :], 0.0).then_inc(s["fills_made"], 1)
            for n in range(SLOTS):
                pool.memset(q_buf[n][:, :, :], 0.0).then_inc(s["fills_made"], 1)
            pool.memset(zeros[:, :, :], 0.0).then_inc(s["fills_made"], 1)
            for n in range(2 * NCH):
                pool.wait_ge(s["part_mid"], n + 1)
                pool.tensor_tensor(split[:, n // 2, n % 2, 2, :], resid[:, n % 2, :], split[:, n // 2, n % 2, 1, :],
                                   ALU.subtract).then_inc(s["part_low"], 1)

            pool.wait_ge(s["gbb_tok_made"], 1)
            pool.wait_ge(s["xn_made"], NT)
            for n in range(CT, NT):
                pool.tensor_tensor(x_sb[:, n, :], x_sb[:, n, :], gbb_tok[:, n // TB, :], ALU.add).then_inc(s["x_biased"], 1)

            def split_max(v_next, pair):
                pool.wait_ge(s["max_done"], 2 + MT * (v_next - 1) + (pair + 1) * MT // 2)
                pool.tensor_tensor(mparts[:, pair, :, :, 0], negmax[:, pair, :, :], zeros[:, :, :],
                                   ALU.add).then_inc(s["max_split"], 1)
                pool.wait_ge(s["max_split"], 4 * v_next - 3 + 2 * pair)
                pool.tensor_tensor(mparts[:, pair, :, :, 1], negmax[:, pair, :, :], mparts[:, pair, :, :, 0],
                                   ALU.subtract).then_inc(s["max_split"], 1)

            def step(i, q):
                if start_of(i, q, LEAD_MA):
                    split_max(stream(i, q, LEAD_MA)[0] + 1, 0)
                if start_of(i, q, LEAD_MB):
                    split_max(stream(i, q, LEAD_MB)[0] + 1, 1)

            pool.wait_ge(s["fills_made"], 5 + SLOTS)
            pipeline(pool, step)

        @block.scalar
        def _(ac):
            ac.dma_start(c_sb[:, :], c).then_inc(s["c_in"], 16)
            for n, w in enumerate((w_q, w_k, w_v, w_o)):
                ac.dma_start(w_nat[:, n, :], w).then_inc(s["wts_in"], 16)
            ac.dma_start(bias_sb[:, :], bias.rearrange("(p o) -> p o", o=1)).then_inc(s["small_in"], 16)
            ac.wait_ge(s["w_turned"], 1)
            ac.activation(c_t[:, 0, :], ps[:, 0, 384:384 + B], ACT.Exp, scale=-1.0).then_inc(s["silu"], 1)
            ac.activation(w_t[:, :, :], ps[:, 0, 0:384].rearrange("p (n d) -> p n d", n=3), ACT.Copy).then_inc(s["w_turned_sb"], 1)
            for b in range(B):
                ac.wait_ge(s["var_ready"], b + 1)
                ac.activation(sd[:, b * TB:(b + 1) * TB], ve[:, b * TB:(b + 1) * TB], ACT.Sqrt).then_inc(s["sd_ready"], 1)
            ac.wait_ge(s["mod_made"], 2)
            for n in range(NCH):
                b = n // HALVES
                ac.wait_ge(s["xn_turned"], n + 1)
                ac.activation(h_t[:, n * CH:(n + 1) * CH], ps[:, 2 + n % 2, :], ACT.Identity,
                              bias=mod[:, 0, b:b + 1], scale=mod[:, 1, b:b + 1]).then_inc(s["h_made"], 1)
                for w in range(2):
                    ac.wait_ge(s["qk_mm"], 2 * n + w + 1)
                    ac.activation(split[:, n, w, 0, :], ps[:, 4 + w, :], ACT.Copy).then_inc(s["part_high"], 1)
                ac.wait_ge(s["fills_made"], 3)
                ac.wait_ge(s["v_mm"], n + 1)
                for t in range(CT):
                    tile = n * CT + t
                    ac.activation(v_all[:, (tile // TB) * (G // B):(tile // TB + 1) * (G // B), tile % TB, :, 0:HD],
                                  ps[:, 6, t * P:(t + 1) * P].rearrange("p (q j d) -> p q j d", q=G // B, j=QH),
                                  ACT.Copy).then_inc(s["v_made"], 1)
                for w in range(2):
                    ac.wait_ge(s["resid_made"], 2 * n + w + 1)
                    ac.activation(split[:, n, w, 1, :], resid[:, w, :], ACT.Copy).then_inc(s["part_mid"], 1)
            ac.wait_ge(s["gbb_made"], B + 1)
            ac.wait_ge(s["gbb_mm"], B)
            ac.activation(gbb_tok[:, :, :], ps[:, 1, 0:B * D].rearrange("p (b d) -> p b d", b=B), ACT.Copy).then_inc(s["gbb_tok_made"], 1)
            ac.wait_ge(s["wo_turned"], 1)
            ac.activation(wo_t[:, :, :], ps[:, 7, 0:B * D].rearrange("p (b d) -> p b d", b=B), ACT.Copy).then_inc(s["exp_done"], 2)

            def copy_max(pair, v_next):
                ac.wait_ge(s["m_turned"], 2 * v_next - 1 + pair)
                ac.activation(mrow_sb[pair][:, :], misc_b[0:2 * MROWS, :], ACT.Copy).then_inc(s["m_copied"], 1)

            def copy_acc(u_next):
                ac.wait_ge(s["value_mm"], PRING + KT * u_next)
                ac.activation(o_sb[:, :], acc, ACT.Copy).then_inc(s["acc_copied"], 1)

            misc_b = misc.bitcast(BF16)[:, 0:CH]

            def step(i, q):
                now = stream(i, q, LEAD_COL)
                for j in range(QH):
                    if now:
                        u, _, kt = now
                        if j == 0:
                            ac.wait_ge(s["value_mm"], KT * u + kt + 1)
                        ac.wait_ge(s["col_mm"], XB * u + kt * QH + j + 1)
                        ac.activation(probs[:, kt % PRING, j, :], col_scores[j % 2], ACT.Exp,
                                      scale=SCALE).then_inc(s["exp_done"], 1)
                    if j == 0 and start_of(i, q, LEAD_ACC):
                        copy_acc(stream(i, q, LEAD_ACC)[0] + 1)
                if start_of(i, q, LEAD_MA):
                    copy_max(0, stream(i, q, LEAD_MA)[0] + 1)
                if start_of(i, q, LEAD_MB):
                    copy_max(1, stream(i, q, LEAD_MB)[0] + 1)

            pipeline(ac, step)

            for n in range(NCH):
                ac.wait_ge(s["hd_turned"], n + 1)
                ac.activation(heads_t[:, n, :], ps[:, 4 + n % 2, :], ACT.Copy).then_inc(s["hd_sb"], 1)
            ac.wait_ge(s["var2"], 1)
            ac.activation(sd[:, 0:CT], ve[:, 0:CT], ACT.Sqrt).then_inc(s["sd2"], 1)
            ac.wait_ge(s["xn2_turned"], 1)
            ac.activation(h2_t[:, :], ps[:, 6, :], ACT.Identity, bias=mod[:, 3, 0:1], scale=mod[:, 4, 0:1]).then_inc(s["h2_made"], 1)

            def gelus(i):
                for n in range(2 * FB):
                    g = i * 2 * FB + n
                    ac.wait_ge(s["ff1_mm"], g + 1)
                    ac.wait_ge(s["gated"], g + 1)
                    ac.activation(act[:, n % 2, :], ps[:, n % 2, :], ACT.Gelu).then_inc(s["gelu_done"], 1)

            with ac.Fori(0, E // 2) as i:
                gelus(i)
            ac.wait_ge(s["ff2_mm"], E * FB)
            ac.activation(y_t[:, :], ps[:, 2, :], ACT.Identity, bias=gbb[:, 0:1], scale=mod[:, 5, 0:1]).then_inc(s["y_sb"], 1)

        @block.vector
        def _(ve_):
            v = ve_
            for n in range(2):
                for par in range(2):
                    v.memset(k_buf[n][HG * par:HG * (par + 1), par::2, :], 1.0).then_inc(s["k_filled"], 1)
                    v.memset(k_buf[n][HG * (1 - par):HG * (2 - par), par::2, :], 0.0).then_inc(s["k_filled"], 1)

            def rstd_chain(a, b, ready_sem, ready, count, chain_sem):
                v.wait_ge(ready_sem, ready)
                v.reciprocal(rs[:, 0, a:b], sd[:, a:b]).then_inc(chain_sem, 1)
                v.wait_ge(chain_sem, count + 1)
                v.tensor_tensor(rs[:, 1, a:b], rs[:, 0, a:b], rs[:, 0, a:b], ALU.mult).then_inc(chain_sem, 1)
                v.wait_ge(chain_sem, count + 2)
                v.tensor_tensor(rs[:, 2, a:b], rs[:, 1, a:b], ve[:, a:b], ALU.mult).then_inc(chain_sem, 1)
                v.wait_ge(chain_sem, count + 3)
                v.tensor_scalar(rs[:, 1, a:b], rs[:, 2, a:b], -0.5, 1.5, ALU.mult, ALU.add).then_inc(chain_sem, 1)
                v.wait_ge(chain_sem, count + 4)
                v.tensor_tensor(rs[:, 3, a:b], rs[:, 0, a:b], rs[:, 1, a:b], ALU.mult).then_inc(chain_sem, 1)
                v.wait_ge(chain_sem, count + 5)

            v.wait_ge(s["silu"], 1)
            v.tensor_scalar(c_t[:, 1, :], c_t[:, 0, :], 1.0, None, ALU.add).then_inc(s["silu"], 1)
            v.wait_ge(s["silu"], 2)
            v.reciprocal(c_t[:, 2, :], c_t[:, 1, :]).then_inc(s["silu"], 1)
            v.wait_ge(s["silu"], 3)
            v.wait_ge(s["w_turned_sb"], 1)
            v.tensor_tensor(c_t[:, 3, :], ps[:, 0, 384:384 + B], c_t[:, 2, :], ALU.mult).then_inc(s["silu"], 1)
            v.wait_ge(s["mod_mm"], 1)
            v.tensor_copy(mod[:, :, :], ps[:, 1, 0:6 * B].rearrange("p (n b) -> p n b", n=6)).then_inc(s["mod_made"], 1)
            v.wait_ge(s["mod_made"], 1)
            v.tensor_scalar(mod[:, 1:5:3, :], mod[:, 1:5:3, :], 1.0, None, ALU.add).then_inc(s["mod_made"], 1)
            done = 0
            for b in range(B):
                for t in range(TB):
                    n = b * TB + t
                    if t % CT == 0:
                        v.wait_ge(x_in[n // CT], 16)
                    v.bn_stats(bn[:, n, :], x_sb[:, n, :]).then_inc(s["stats"], 1)
                    done += 1
                for t in range(TB):
                    n = b * TB + t
                    v.wait_ge(s["stats"], done - TB + t + 1)
                    v.bn_aggr(mv[:, n, :], bn[:, n, :]).then_inc(s["stats"], 1)
                done += TB
                v.wait_ge(s["stats"], done)
                v.tensor_scalar(ve[:, b * TB:(b + 1) * TB], mv[:, b * TB:(b + 1) * TB, 1], EPS, None, ALU.add).then_inc(s["var_ready"], 1)
                rstd_chain(b * TB, (b + 1) * TB, s["sd_ready"], b + 1, 5 * b, s["rstd"])
                for t in range(TB):
                    n = b * TB + t
                    v.tensor_scalar(xn[:, n, :], x_sb[:, n, :], mv[:, n, 0:1], rs[:, 3, n:n + 1],
                                    ALU.subtract, ALU.mult).then_inc(s["xn_made"], 1)
            v.tensor_scalar(sgn[:, :, :], mod[:, 2:6:3, :], 0.0, 2.0, ALU.is_ge, ALU.mult).then_inc(s["gates_made"], 1)
            v.scalar_tensor_tensor(out=mag[:, :, :], in0=mod[:, 2:6:3, :], scalar=-1.0, in1=mod[:, 2:6:3, :],
                                   op0=ALU.mult, op1=ALU.max).then_inc(s["gates_made"], 1)
            v.wait_ge(s["gates_made"], 2)
            v.tensor_scalar(mag[:, :, :], mag[:, :, :], 0.25, None, ALU.max).then_inc(s["gates_made"], 1)
            v.wait_ge(s["gates_made"], 3)
            v.scalar_tensor_tensor(out=mod[:, 2:6:3, :], in0=sgn[:, :, :], scalar=-1.0, in1=mag[:, :, :],
                                   op0=ALU.add, op1=ALU.mult).then_inc(s["gates_made"], 1)
            v.wait_ge(s["gates_made"], 4)
            v.wait_ge(s["wts_in"], 64)
            for b in range(B):
                v.tensor_scalar(wo_g[:, b, :], w_nat[:, 3, :], mod[:, 2, b:b + 1], None, ALU.mult).then_inc(s["wo_made"], 1)
            v.wait_ge(s["small_in"], 48)
            v.tensor_scalar(gbb[:, :], mod[:, 5, :], bias_sb[:, 0:1], None, ALU.mult).then_inc(s["gbb_made"], 1)
            v.wait_ge(s["gbb_made"], 1)
            v.wait_ge(s["fills_made"], 2)
            for b in range(B):
                v.tensor_scalar(gbb_w[:, b, :], ones[:, :], gbb[:, b:b + 1], None, ALU.mult).then_inc(s["gbb_made"], 1)
            for n in range(2 * NCH):
                v.wait_ge(s["part_high"], n + 1)
                if n >= 2:
                    v.wait_ge(s["part_low"], n - 1)
                v.tensor_tensor(resid[:, n % 2, :], ps[:, 4 + n % 2, :], split[:, n // 2, n % 2, 0, :],
                                ALU.subtract).then_inc(s["resid_made"], 1)
            v.tensor_copy(idx_f[:, :, :], idx_i[:, :, :]).then_inc(s["gate_made"], 1)
            v.wait_ge(s["gate_made"], 1)
            for e in range(E):
                v.scalar_tensor_tensor(out=hit[:, e, :, :], in0=idx_f[:, :, :], scalar=float(e), in1=ew[:, :, :],
                                       op0=ALU.is_equal, op1=ALU.mult).then_inc(s["gate_made"], 1)
            v.wait_ge(s["gate_made"], 1 + E)
            v.tensor_reduce(gate[:, :, :].rearrange("p t e -> p e t"), hit[:, :, :, :], AX.X, ALU.add).then_inc(s["gate_made"], 1)
            v.wait_ge(s["gate_turned"], 1)
            v.tensor_copy(gate_t[:, :], ps[0:E, 0, :]).then_inc(s["gate_t_sb"], 1)
            v.wait_ge(s["v_made"], NT)
            v.memset(acc, 0.0).then_inc(s["value_mm"], PRING)
            v.wait_ge(s["gate_t_sb"], 1)
            v.tensor_copy(o_rec[:, 0, 0:1], ones[:, 0:1]).then_inc(s["max_done"], 2)

            def row_max(v_next, m):
                v.wait_ge(s["row_mm"], MT * (v_next - 1) + m + 1)
                j, t = m // CT, m % CT
                v.tensor_reduce(negmax[:, j // 2, t, j % 2:j % 2 + 1], row_scores[m % 2].rearrange("p a k -> p (a k)"),
                                AX.X, ALU.max, negate=True).then_inc(s["max_done"], 1)

            def normalise(u_next, b, quad, half):
                o = misc.rearrange("p (t j w) -> p t j w", t=CT, j=QH)
                v.wait_ge(s["o_turned"], u_next)
                v.reciprocal(o_rec[:, :, :], o[:, :, :, HD]).then_inc(s["o_rec_made"], 1)
                v.wait_ge(s["o_rec_made"], u_next)
                v.tensor_tensor(heads[:, b, half, :, bass.ds(quad * QH * HD, QH * HD)].rearrange("p t (j d) -> p t j d", j=QH), o[:, :, :, 0:HD],
                                o_rec[:, :, :].rearrange("p t (j o) -> p t j o", o=1).to_broadcast([P, CT, QH, HD]),
                                ALU.mult).then_inc(s["o_made"], 1)

            def step(i, q):
                now = stream(i, q, LEAD_ROW)
                if now:
                    for m in range(2 * now[2], 2 * now[2] + 2):
                        row_max(now[0] + 1, m)
                if start_of(i, q, 0):
                    u, t, _ = stream(i, q, 0)
                    normalise(u + 1, i // 2, i % 2 * 2 + t // 2, t % 2)

            pipeline(v, step)

            for n in range(NCH):
                v.wait_ge(s["proj_mm"], n + 1)
                if n == 1:
                    v.wait_ge(s["x_biased"], NT - CT)
                for t in range(CT):
                    v.tensor_tensor(res[:, n * CT + t, :], ps[:, n % 2, t * P:(t + 1) * P], x_sb[:, n * CT + t, :],
                                    ALU.add).then_inc(s["x1_made"], 1)
                if n == 0:
                    for t in range(CT):
                        v.wait_ge(s["x1_made"], t + 1)
                        v.bn_stats(bn[:, t, :], res[:, t, :]).then_inc(s["st2"], 1)
                    for t in range(CT):
                        v.wait_ge(s["st2"], t + 1)
                        v.bn_aggr(mv[:, t, :], bn[:, t, :]).then_inc(s["st2"], 1)
                    v.wait_ge(s["st2"], 2 * CT)
                    v.tensor_scalar(ve[:, 0:CT], mv[:, 0:CT, 1], EPS, None, ALU.add).then_inc(s["var2"], 1)
                    rstd_chain(0, CT, s["sd2"], 1, 0, s["rstd2"])
                    for t in range(CT):
                        v.tensor_scalar(xn[:, t, :], res[:, t, :], mv[:, t, 0:1], rs[:, 3, t:t + 1],
                                        ALU.subtract, ALU.mult).then_inc(s["xn2"], 1)
            v.wait_ge(s["gate_b_in"], 16)
            v.tensor_copy(o_rec[:, 0, 0:1], ones[:, 0:1]).then_inc(s["gated"], 2)

            def gates(i):
                for n in range(2 * FB):
                    g = i * 2 * FB + n
                    v.wait_ge(s["gelu_done"], g + 1)
                    v.tensor_tensor(acg[:, n % 2, :], act[:, n % 2, :], gate_b[:, i * 2 + n // FB, :], ALU.mult).then_inc(s["gated"], 1)

            with v.Fori(0, E // 2) as i:
                gates(i)
            v.wait_ge(s["y_turned"], 1)
            for t in range(CT):
                v.tensor_tensor(res[:, t, :], ps[:, 3, t * P:(t + 1) * P], res[:, t, :], ALU.add).then_inc(s["y_added"], 1)

        @block.tensor
        def _(pe):
            pe.wait_ge(s["ident_made"], 2)
            pe.wait_ge(s["wts_in"], 64)
            pe.wait_ge(s["c_in"], 16)
            for n in range(3):
                pe.transpose(ps[:, 0, n * P:(n + 1) * P], w_nat[:, n, :], ident[:, :])
            pe.transpose(ps[:, 0, 384:384 + B], c_sb[:, :], ident[0:B, 0:B]).then_inc(s["w_turned"], 1)
            pe.wait_ge(s["silu"], 4)
            pe.wait_ge(s["wmod_in"], 16)
            for n in range(6):
                mm = pe.matmul(ps[:, 1, n * B:(n + 1) * B], wmod_sb[:, n * D:(n + 1) * D], c_t[:, 3, :], start=True, stop=True)
            mm.then_inc(s["mod_mm"], 1)
            pe.wait_ge(s["w_turned_sb"], 1)

            def turn_xn(n):
                for t in range(CT):
                    pe.wait_ge(s["xn_made"], n * CT + t + 1)
                    mm = pe.transpose(ps[:, 2 + n % 2, t * P:(t + 1) * P], xn[:, n * CT + t, :], ident[:, :])
                mm.then_inc(s["xn_turned"], 1)

            turn_xn(0)
            for n in range(NCH):
                if n + 1 < NCH:
                    if n >= 1:
                        pe.wait_ge(s["h_made"], n)
                    turn_xn(n + 1)
                pe.wait_ge(s["h_made"], n + 1)
                for w in range(2):
                    if n >= 1:
                        pe.wait_ge(s["resid_made"], 2 * n - 1 + w)
                    pe.matmul(ps[:, 4 + w, :], w_t[:, w, :], h_t[:, n * CH:(n + 1) * CH], start=True, stop=True).then_inc(s["qk_mm"], 1)
                if n >= 1:
                    pe.wait_ge(s["v_made"], n * CT)
                for t in range(CT):
                    mm = pe.matmul(ps[:, 6, t * P:(t + 1) * P], h_t[:, (n * CT + t) * P:(n * CT + t + 1) * P], w_t[:, 2, :],
                                   start=True, stop=True)
                mm.then_inc(s["v_mm"], 1)
            pe.wait_ge(s["gbb_made"], 1 + B)
            for b in range(B):
                pe.matmul(ps[:, 1, b * D:(b + 1) * D], gbb_w[:, b, :], ident[:, :], start=True, stop=True).then_inc(s["gbb_mm"], 1)
            pe.wait_ge(s["wo_made"], B)
            for b in range(B):
                mm = pe.transpose(ps[:, 7, b * D:(b + 1) * D], wo_g[:, b, :], ident[:, :])
            mm.then_inc(s["wo_turned"], 1)
            pe.wait_ge(s["gate_made"], 2 + E)
            for t in range(CT):
                mm = pe.transpose(ps[0:E, 0, t * P:(t + 1) * P], gate[:, t, :], ident[:, :])
            mm.then_inc(s["gate_turned"], 1)
            pe.wait_ge(s["exp_done"], 2)
            pe.wait_ge(s["h_made"], NCH)
            pe.wait_ge(s["value_mm"], PRING)

            misc_b = misc.bitcast(BF16)[:, 0:CH]

            def row_tile(i, q, m):
                u, buf, _ = stream(i, q, LEAD_ROW)
                j, t = m // CT, m % CT
                if m == 0:
                    loads = i + (q + LEAD_ROW) // STEPS + 1
                    pe.wait_ge(q_in[buf], 64 * loads)
                    if buf % 2 == 0:
                        pe.wait_ge(k_in[buf // 2], 32 * loads)
                pe.wait_ge(s["max_done"], MT * u + m + 1)
                for a in range(S // 512):
                    mm = pe.matmul(row_scores[m % 2][:, a, :], q_buf[buf][:, j // 2, t * P:(t + 1) * P],
                                   k_buf[buf // 2][:, j, a * 512:(a + 1) * 512], start=True, stop=True)
                mm.then_inc(s["row_mm"], 1)

            def col_tile(i, q, j):
                u, buf, kt = stream(i, q, LEAD_COL)
                if kt == 0 and j == 0:
                    pe.wait_ge(s["m_rows_a"], 32 * (u + 1))
                if kt == 0 and j == 2:
                    pe.wait_ge(s["m_rows_b"], 32 * (u + 1))
                pe.wait_ge(s["exp_done"], XB * u + kt * QH + j + 1)
                pe.matmul(col_scores[j % 2], k_buf[buf // 2][:, j, kt * P:(kt + 1) * P], q_buf[buf][:, j // 2, :],
                          start=True, stop=True).then_inc(s["col_mm"], 1)

            def turn_max(v_next, pair):
                pe.wait_ge(s["max_split"], 4 * v_next - 2 + 2 * pair)
                for t in range(CT):
                    mm = pe.transpose(misc_b[0:2 * MROWS, t * P:(t + 1) * P],
                                      mparts[:, pair, t, :, :].rearrange("p j w -> p (j w)"), ident_b[:, :])
                mm.then_inc(s["m_turned"], 1)

            def turn_out(u_next):
                pe.wait_ge(s["acc_copied"], u_next)
                for t in range(CT):
                    mm = pe.transpose(misc[:, t * P:(t + 1) * P], o_sb[:, t * P:(t + 1) * P], ident[:, :])
                mm.then_inc(s["o_turned"], 1)

            def value_tile(i, q):
                u, t, kt = stream(i, q, LEAD_VALUE)
                pe.wait_ge(s["exp_done"], 2 + XB * u + QH * (kt + 1))
                if kt == 0:
                    if t % 2 == 0:
                        pe.wait_ge(v_in[t // 2], 16 * (i + (q + LEAD_VALUE) // STEPS + 1))
                    if type(u) is not int or u > 0:
                        pe.wait_ge(s["acc_copied"], u)
                for j in range(QH):
                    mm = pe.matmul(acc[32 * j:32 * j + VC, :], v_st[:, t // 2, kt, j, :], probs[:, kt % PRING, j, :],
                                   start=(kt == 0), stop=(kt == KT - 1))
                mm.then_inc(s["value_mm"], 1)

            def step(i, q):
                col, row, value = stream(i, q, LEAD_COL), stream(i, q, LEAD_ROW), stream(i, q, LEAD_VALUE)
                if col:
                    col_tile(i, q, 0)
                    col_tile(i, q, 1)
                if row:
                    row_tile(i, q, 2 * row[2])
                if col:
                    col_tile(i, q, 2)
                if value:
                    value_tile(i, q)
                if col:
                    col_tile(i, q, 3)
                if start_of(i, q, 0):
                    u = stream(i, q, 0)[0]
                    pe.wait_ge(s["m_copied"], 2 * u + 5 if type(u) is not int else min(2 * u + 5, 2 * U))
                    if type(u) is int and u > U - 2:
                        pe.wait_ge(s["o_made"], u)
                    turn_out(u + 1)
                if row:
                    row_tile(i, q, 2 * row[2] + 1)
                if start_of(i, q, LEAD_MA):
                    u = stream(i, q, LEAD_MA)[0]
                    if type(u) is not int or u > 0:
                        pe.wait_ge(s["m_copied"], 2 * u)
                    turn_max(u + 1, 0)
                if start_of(i, q, LEAD_MB):
                    u = stream(i, q, LEAD_MB)[0]
                    pe.wait_ge(s["m_copied"], 2 * u + 1)
                    if type(u) is not int or u > 1:
                        pe.wait_ge(s["o_made"], u - 1)
                    turn_max(u + 1, 1)

            pipeline(pe, step)

            def turn_heads(n):
                b, half = n // HALVES, n % HALVES
                if n >= 2:
                    pe.wait_ge(s["hd_sb"], n - 1)
                for t in range(CT):
                    mm = pe.transpose(ps[:, 4 + n % 2, t * P:(t + 1) * P], heads[:, b, half, t, :],
                                      ident[:, :])
                mm.then_inc(s["hd_turned"], 1)

            pe.wait_ge(s["o_made"], U)
            turn_heads(0)
            for n in range(NCH):
                if n + 1 < NCH:
                    turn_heads(n + 1)
                pe.wait_ge(s["hd_sb"], n + 1)
                if n >= 2:
                    pe.wait_ge(s["x1_made"], (n - 1) * CT)
                for t in range(CT):
                    mm = pe.matmul(ps[:, n % 2, t * P:(t + 1) * P], heads_t[:, n, t * P:(t + 1) * P], wo_t[:, n // HALVES, :],
                                   start=True, stop=True)
                mm.then_inc(s["proj_mm"], 1)
            for t in range(CT):
                pe.wait_ge(s["xn2"], t + 1)
                mm = pe.transpose(ps[:, 6, t * P:(t + 1) * P], xn[:, t, :], ident[:, :])
            mm.then_inc(s["xn2_turned"], 1)
            pe.wait_ge(s["h2_made"], 1)
            pe.wait_ge(s["x1_made"], NT)

            def ff1(i, n, count):
                if n % FB == 0:
                    pe.wait_ge(s[f"w1_in{n // FB}"], 16 * (i + 1))
                pe.matmul(ps[:, n % 2, :], w1_sb[n // FB][:, (n % FB) * P:(n % FB + 1) * P], h2_t[:, :],
                          start=True, stop=True).then_inc(s["ff1_mm"], 1)

            def ff2(i, n, start, stop):
                if n % FB == 0:
                    pe.wait_ge(s[f"w2_in{n // FB}"], 16 * (i + 1))
                pe.wait_ge(s["gated"], i * 2 * FB + n + 3)
                pe.matmul(ps[:, 2, :], w2_sb[n // FB][:, n % FB, :], acg[:, n % 2, :], start=start, stop=stop,
                          skip_group_check=True).then_inc(s["ff2_mm"], 1)

            def experts(i, first, last):
                for n in range(2 * FB):
                    if not (last and n == 2 * FB - 1):
                        if n + 1 < 2 * FB:
                            ff1(i, n + 1, None)
                        else:
                            ff1(i + 1, 0, None)
                    ff2(i, n, first and n == 0, last and n == 2 * FB - 1)

            ff1(0, 0, None)
            experts(0, True, False)
            with pe.Fori(1, E // 2 - 1) as i:
                experts(i, False, False)
            experts(E // 2 - 1, False, True)
            pe.wait_ge(s["y_sb"], 1)
            for t in range(CT):
                mm = pe.transpose(ps[:, 3, t * P:(t + 1) * P], y_t[:, t * P:(t + 1) * P], ident[:, :])
            mm.then_inc(s["y_turned"], 1)


LEAD_ACC = 1
LEAD_VALUE = 9
LEAD_COL = LEAD_VALUE + 2
LEAD_MB = LEAD_COL + 3
LEAD_MA = LEAD_MB + 4
LEAD_ROW = LEAD_MB + 8
LEAD_LOAD_V = 24
LEAD_LOAD = 27

_INS = ["L0_attn_x", "L0_attn_w_q", "L0_attn_w_k", "L0_attn_w_v", "L0_attn_w_o", "L0_ffn_expert_weights",
        "L0_ffn_expert_indices", "L0_ffn_w1", "L0_ffn_w2", "L0_ffn_bias", "L0_c", "L0_wmod"]


def kernel(**inputs):
    import numpy as _np
    import concourse.bacc as _bacc
    from concourse import mybir as _mybir
    from concourse.bass_utils import run_bass_kernel_spmd as _run

    nc = _bacc.Bacc("TRN2", target_bir_lowering=False, num_devices=1)
    arrays, args = {}, []
    for name in _INS:
        a = _np.ascontiguousarray(inputs[name])
        arrays[f"in_{name}_dram"] = a
        args.append(nc.dram_tensor(f"in_{name}_dram", a.shape, _mybir.dt.from_np(a.dtype), kind="ExternalInput").ap())
    out = nc.dram_tensor("out_dram", inputs["L0_attn_x"].shape, _mybir.dt.float32, kind="ExternalOutput").ap()
    adaln_block(nc, *args, out)
    r = _run(nc, [arrays], core_ids=[0])
    return r.results[0]["out_dram"]
```

```python
from contextlib import ExitStack

import concourse.bass as bass
from concourse import mybir

F32 = mybir.dt.float32
BF16 = mybir.dt.bfloat16
I32 = mybir.dt.int32
ALU = mybir.AluOpType
ACT = mybir.ActivationFunctionType
AX = mybir.AxisListType

P = 128
EPS = 1e-5


def adaln_block(nc, x, w_q, w_k, w_v, w_o, expert_weights, expert_indices, w1, w2, bias, c, wmod, out):
    B, S, D = x.shape
    H, HD = 16, 8
    assert D == P and H * HD == D
    T = B * S
    NT = T // P
    TB = S // P
    CH = 512
    NCH = T // CH
    CT = CH // P
    E, _, FF = w1.shape
    FT, TOPK = expert_indices.shape
    assert FT == CH
    FB = FF // P
    PARTS = 3
    TERMS = 6
    ROWS = TERMS * HD
    MROWS = 2
    HG = 64
    QH = 4
    G = B * H // QH
    HALVES = S // CH
    U = G * HALVES
    SLOTS = 4
    KT = S // P
    VC = HD + 1
    SCALE = float(HD) ** -0.5
    XB = KT * QH
    MT = QH * CT
    CHAIN = 11
    RSQRT_BITS = 0x5F3759DF
    WARM = 40
    FRING = 4
    AHEAD = 2
    PRING = 4

    ctx = ExitStack()
    with ctx:
        def sb(name, shape, dt=F32):
            return ctx.enter_context(nc.sbuf_tensor(name, shape, dt))

        def sem(name):
            return ctx.enter_context(nc.semaphore(name))

        q_rows = nc.dram_tensor("q_rows", [B * H, ROWS, S], BF16).ap()
        k_rows = nc.dram_tensor("k_rows", [B * H, ROWS, S], BF16).ap()
        gate_rows = nc.dram_tensor("gate_rows", [E, FT], F32).ap()

        x_sb = sb("x_sb", [P, NT, D])
        xn = sb("xn", [P, NT, D])
        h_t = sb("h_t", [P, T])
        w_nat = sb("w_nat", [P, 4, D])
        w_t = sb("w_t", [P, 3, D])
        wo_g = sb("wo_g", [P, B, D])
        wo_t = sb("wo_t", [P, B, D])
        wmod_sb = sb("wmod_sb", [P, 6 * D])
        c_sb = sb("c_sb", [B, D])
        c_t = sb("c_t", [P, 4, B])
        mod = sb("mod", [P, 6, B])
        sgn = sb("sgn", [P, 2, B])
        mag = sb("mag", [P, 2, B])
        bias_sb = sb("bias_sb", [P, 1])
        gbb = sb("gbb", [P, B])
        gbb_w = sb("gbb_w", [P, B, P])
        gbb_tok = sb("gbb_tok", [P, B, D])
        ident = sb("ident", [P, P])
        ident_b = sb("ident_b", [P, P], BF16)
        ones = sb("ones", [P, P])
        bn = sb("bn", [P, NT, 6])
        mv = sb("mv", [P, NT, 2])
        ve = sb("ve", [P, NT])
        rs = sb("rs", [P, 4, NT])
        split = sb("split", [P, NCH, 2, PARTS, CH], BF16)
        resid = sb("resid", [P, 4, CH])
        v_all = sb("v_all", [P, G, KT, QH, VC])
        v_st = sb("v_st", [P, 2, KT, QH, VC])
        q_buf = [sb(f"q_buf{n}", [P, 2, CH], BF16) for n in range(SLOTS)]
        k_buf = [sb(f"k_buf{n}", [P, QH, S], BF16) for n in range(2)]
        negmax = sb("negmax", [P, 2, 2, CT])
        one_rows = sb("one_rows", [MROWS, 2, S], BF16)
        zero_rows = sb("zero_rows", [MROWS, 2, CH], BF16)
        zeros = sb("zeros", [P, 2, CT])
        mparts = sb("mparts", [P, 2, 2, MROWS, CT], BF16)
        mrow_sb = [sb(f"mrow_sb{n}", [2 * MROWS * CT, P], BF16) for n in range(2)]
        probs = sb("probs", [P, PRING, QH, CH])
        o_sb = sb("o_sb", [P, CH])
        o_rec = sb("o_rec", [P, CT, QH])
        heads = sb("heads", [P, B, HALVES, CT, D])
        heads_t = sb("heads_t", [P, NCH, CH])
        idx_i = sb("idx_i", [P, CT, TOPK], I32)
        idx_f = sb("idx_f", [P, CT, TOPK])
        ew = sb("ew", [P, CT, TOPK])
        hit = sb("hit", [P, E, CT, TOPK])
        gate = sb("gate", [P, CT, E])
        gate_t = sb("gate_t", [E, FT])
        gate_b = sb("gate_b", [P, E, FT])
        h2_t = sb("h2_t", [P, FT])
        w1_sb = [sb(f"w1_sb{n}", [P, FF]) for n in range(2)]
        w2_sb = [sb(f"w2_sb{n}", [P, FB, D]) for n in range(2)]
        y_t = sb("y_t", [P, FT])
        credit = sb("credit", [P, 3])
        act = probs[:, 0, :, :]
        acg = probs[:, 1, :, :]
        res = x_sb

        ps = ctx.enter_context(nc.psum_tensor("ps", [P, 8, 512], F32))
        row_scores = [ps[:, 0:2, :], ps[:, 2:4, :]]
        acc = ps[:, 6, :]
        misc = ps[:, 7, :]
        ff1_out = [ps[:, n, :] for n in (0, 1, 6, 7)]
        ff2_out = ps[:, 5, :]

        names = [
                 "ident_cleared", "ident_made", "fills_made", "k_filled", "q_cleared", "v_ones", "ones_made",
                 "c_in", "wts_in", "wo_in", "wmod_in", "small_in",
                 "c_turned", "w_turned", "w_turned_sb", "silu", "silu_dve", "mod_mm", "mod_made",
                 "stats", "var_ready", "rstd", "xn_made", "xn_turned", "h_made", "qk_mm", "v_mm",
                 "part_high", "resid_made", "part_mid", "part_low", "part_low2", "resid_made2", "proj_copied", "v_made",
                 "gates_made", "wo_made", "wo_turned_sb", "gate_made", "gate_turned", "gate_t_sb", "gate_spilled",
                 "gate_b_in", "gbb_made", "gates_turned", "gbb_tok_made", "x_biased",
                 "row_mm", "max_done", "max_split", "m_turned", "m_copied", "m_rows_a", "m_rows_b",
                 "col_mm", "exp_done", "value_mm", "acc_copied", "acc_copied_v", "o_turned", "o_rec_made", "o_made",
                 "hd_turned", "hd_sb", "proj_mm", "x1_made", "st2", "var2", "rstd2", "xn2", "xn2_turned", "h2_made",
                 "w1_in0", "w1_in1", "w2_in0", "w2_in1", "ff1_mm", "gelu_done", "gated", "ff2_mm", "y_sb", "y_turned",
                 "y_added", "stored"]
        s = {n: sem(n) for n in names}
        x_in = [sem(f"x_in{n}") for n in range(NCH)]
        q_in = [sem(f"q_in{n}") for n in range(SLOTS)]
        spilled = [sem(f"spilled{n}") for n in range(8)]
        v_in = [sem(f"v_in{n}") for n in range(2)]
        k_in = [sem(f"k_in{n}") for n in range(2)]

        block = ctx.enter_context(nc.Block())

        x_rows = x.rearrange("b (t p) d -> p (b t) d", p=P)
        out_rows = out.rearrange("b (t p) d -> p (b t) d", p=P)
        q_write = q_rows.rearrange("(b h) (d t) n -> b (h d) t n", b=B, t=TERMS)
        k_write = k_rows.rearrange("(b h) (d t) n -> b (h d) t n", b=B, t=TERMS)

        STEPS = SLOTS * KT

        PROJ = [(0, 1, 4), (0, 0, 5), (1, 1, 0), (1, 0, 6), (2, 1, 5), (3, 1, 4), (2, 0, 5), (3, 0, 4)]
        NP0 = 4
        V_BANK = [7, 4, 6, 5]
        T_BANK = [2, 3, 6, 6]

        PIECES = {-22: ("proj", 4), -21: ("turn", 3), -20: ("proj", 5), -19: ("proj", 6), -16: ("proj", 7),
                  -15: ("values", 2), -13: ("clear", 0), -4: ("gates", 0), -3: ("gate rows", 0)}
        PREPARE = {-12: 0, -11: 1, -10: 2, -9: 3, -8: 4, -7: 5, -6: 6}

        TAIL = STEPS - LEAD_ROW + 1
        TAIL_PIECES = {TAIL: ("turn", 0), TAIL + 1: ("proj", 0), TAIL + 2: ("turn", 1), TAIL + 3: ("proj", 1),
                       TAIL + 6: ("turn", 2), TAIL + 7: ("proj", 2), TAIL + 9: ("norm", 0), TAIL + 12: ("ff1", 0)}

        def col_bank(i, q, j):
            return (4, 5, 0, 1)[j] if in_tail(i, q) else 4 + j % 2

        def in_tail(i, q):
            return type(i) is int and i > 0 and q >= TAIL

        def tail_piece(i, q):
            return TAIL_PIECES.get(q, (None, 0)) if in_tail(i, q) else (None, 0)

        def stream(i, q, lead):
            n = q + lead
            unit = i * SLOTS + n // KT
            if n < 0 or (type(unit) is int and unit >= U):
                return None
            return unit, n // KT % SLOTS, n % KT

        def start_of(i, q, lead):
            found = stream(i, q, lead)
            return found if found is not None and found[2] == 0 else None

        def pipeline(eng, step):
            for q in range(-LEAD_ROW, 0):
                step(0, q)
            with eng.Fori(0, U // SLOTS - 1) as i:
                for q in range(STEPS):
                    step(i, q)
            for q in range(STEPS):
                step(U // SLOTS - 1, q)

        FIRST = slice(0, QH * HD)
        REST = slice(QH * HD, D)

        def spill(eng, n, ready, channels=slice(0, D)):
            chunk, is_k, _ = PROJ[n]
            b, at = chunk // HALVES, (chunk % HALVES) * CH
            for at_term, k, part in ((0, 3, 0), (3, 2, 1), (5, 1, 2)) if is_k else ((5, 1, 0), (3, 2, 1), (0, 3, 2)):
                if ready[part]:
                    eng.wait_ge(*ready[part])
                if is_k:
                    src = split[channels, chunk, 1, part:part + 1, :].to_broadcast([channels.stop - channels.start, k, CH])
                else:
                    src = split[channels, chunk, 0, 0:k, :]
                rows = (k_write if is_k else q_write)[b][channels, at_term:at_term + k, at:at + CH]
                eng.dma_start(rows, src).then_inc(spilled[n], 16)

        def load_q(eng, buf, g, half, first=False):
            for par in range(2):
                src = q_rows.rearrange("(g r two) w n -> g two w r n", r=2, two=2)[g, par][:, :, half * CH:(half + 1) * CH]
                eng.dma_start(q_buf[buf][HG * par:HG * par + ROWS, :, :], src).then_inc(q_in[buf], 16)
                if not first:
                    eng.dma_start(q_buf[buf][HG * par + ROWS:HG * par + ROWS + MROWS, :, :],
                                  zero_rows[:, :, :]).then_inc(q_in[buf], 16)

        def load_k(eng, buf, g):
            for par in range(2):
                src = k_rows.rearrange("(g r two) w n -> g two w r n", r=2, two=2)[g, par]
                eng.dma_start(k_buf[buf][HG * par:HG * par + ROWS, par::2, :], src).then_inc(k_in[buf], 16)

        def stage_values(eng, buf, g):
            eng.dma_start(v_st[:, buf, :, :, :], v_all[:, g, :, :, :]).then_inc(v_in[buf], 16)

        def send_max_rows(eng, v_next, buf, pair):
            eng.wait_ge(s["m_copied"], 2 * v_next - 1 + pair)
            for par in range(2):
                eng.dma_start(q_buf[buf][HG * par + ROWS:HG * par + ROWS + MROWS, pair, :],
                              mrow_sb[pair][MROWS * CT * par:MROWS * CT * (par + 1), :]).then_inc(
                                  s["m_rows_b" if pair else "m_rows_a"], 16)

        @block.sync
        def _(sp):
            for n in range(NCH):
                sp.dma_start(x_sb[:, n * CT:(n + 1) * CT, :], x_rows[:, n * CT:(n + 1) * CT, :]).then_inc(x_in[n], 16)
                if n == 1:
                    sp.dma_start(wmod_sb[:, :], wmod).then_inc(s["wmod_in"], 16)
            ew_v = expert_weights.rearrange("(t p) k -> p t k", p=P)
            ei_v = expert_indices.rearrange("(t p) k -> p t k", p=P)
            sp.dma_start(ew[:, :, :], ew_v).then_inc(s["small_in"], 16)
            sp.dma_start(idx_i[:, :, :], ei_v).then_inc(s["small_in"], 16)
            sp.dma_start(w_nat[:, 3, :], w_o).then_inc(s["wo_in"], 16)
            sp.dma_start(bias_sb[:, :], bias.rearrange("(p o) -> p o", o=1)).then_inc(s["small_in"], 16)
            sp.wait_ge(s["fills_made"], 3)
            for n in range(2):
                for par in range(2):
                    sp.dma_start(k_buf[n][HG * par + ROWS:HG * par + ROWS + MROWS, par::2, :],
                                 one_rows[:, :, :]).then_inc(s["k_filled"], 16)
            for n in range(NP0 - 1):
                spill(sp, n, [(s["part_high"], n + 1), (s["part_mid"], n + 1), (s["part_low"], n + 1)], FIRST)
            sp.wait_ge(spilled[1], 48)
            sp.wait_ge(s["q_cleared"], SLOTS + 1)
            load_q(sp, 0, 0, 0, first=True)
            sp.wait_ge(spilled[0], 48)
            sp.wait_ge(spilled[2], 48)
            load_k(sp, 0, 0)
            spill(sp, 3, [(s["part_low"], 4), None, None])
            for n in range(NP0 - 1):
                spill(sp, n, [None, None, None], REST)
            sp.wait_ge(spilled[3], 48)
            load_q(sp, 1, 0, 1, first=True)
            for n in range(NP0 - 1):
                sp.wait_ge(spilled[n], 96)
            load_k(sp, 1, 1)
            load_q(sp, 2, 1, 0, first=True)
            load_q(sp, 3, 1, 1, first=True)
            sp.wait_ge(s["v_made"], NT // 2)
            stage_values(sp, 0, 0)
            stage_values(sp, 1, 1)

            w1_v = w1.rearrange("e k f -> k e f")
            w2_v = w2.rearrange("e (b p) d -> p e b d", p=P)

            def step(i, q):
                if type(i) is int and i > 0 and q == TAIL:
                    sp.wait_ge(s["gate_spilled"], 16)
                    sp.dma_start(gate_b[:, :, :], gate_rows.rearrange("(o e) t -> o e t", o=1).to_broadcast(
                        [P, E, FT])).then_inc(s["gate_b_in"], 16)
                    for n in range(2):
                        sp.dma_start(w1_sb[n][:, :], w1_v[:, n, :]).then_inc(s[f"w1_in{n}"], 16)
                        sp.dma_start(w2_sb[n][:, :, :], w2_v[:, n, :, :]).then_inc(s[f"w2_in{n}"], 16)
                if start_of(i, q, LEAD_MA):
                    u, t, _ = stream(i, q, LEAD_MA)
                    send_max_rows(sp, u + 1, t, 0)
                if start_of(i, q, LEAD_MB):
                    u, t, _ = stream(i, q, LEAD_MB)
                    send_max_rows(sp, u + 1, t, 1)
                if type(i) is int and q == -12:
                    for n in range(4, 8):
                        spill(sp, n, [(s["part_low2"], n - 3), None, None])
                if q == -1:
                    for n in range(4, 8):
                        sp.wait_ge(spilled[n], 48)
                    sp.wait_ge(s["gate_t_sb"], 1)
                    sp.dma_start(gate_rows[:, :], gate_t[:, :]).then_inc(s["gate_spilled"], 16)
                load = start_of(i, q, LEAD_LOAD)
                if load and not (type(load[0]) is int and load[0] < SLOTS):
                    u, t, _ = load
                    g = i * 2 + (q + LEAD_LOAD) // KT // 2
                    sp.wait_ge(s["col_mm"], (u - 3) * XB)
                    load_q(sp, t, g, t % 2)
                    if t % 2 == 0:
                        sp.wait_ge(s["col_mm"], (u - 2) * XB)
                        load_k(sp, t // 2, g)
                load = start_of(i, q, LEAD_LOAD_V)
                if load and load[1] % 2 == 0 and not (type(load[0]) is int and load[0] < SLOTS):
                    u, t, _ = load
                    sp.wait_ge(s["value_mm"], PRING + KT * (u - 2))
                    stage_values(sp, t // 2, i * 2 + (q + LEAD_LOAD_V) // KT // 2)

            pipeline(sp, step)

            for n in range(1, NCH):
                sp.wait_ge(s["x1_made"], n + 1)
                sp.dma_start(out_rows[:, n * CT:(n + 1) * CT, :], res[:, n * CT:(n + 1) * CT, :]).then_inc(s["stored"], 16)
            with sp.Fori(0, E // 2 - 1) as i:
                for n in range(2):
                    sp.wait_ge(s["ff1_mm"], (i * 2 + n + 1) * FB)
                    sp.dma_start(w1_sb[n][:, :], w1_v[:, i * 2 + n + 2, :]).then_inc(s[f"w1_in{n}"], 16)
                    sp.wait_ge(s["ff2_mm"], (i * 2 + n + 1) * FB)
                    sp.dma_start(w2_sb[n][:, :, :], w2_v[:, i * 2 + n + 2, :, :]).then_inc(s[f"w2_in{n}"], 16)
            for n in range(2):
                half = slice(n * CT // 2, (n + 1) * CT // 2)
                sp.wait_ge(s["y_added"], n + 1)
                sp.dma_start(out_rows[:, half, :], res[:, half, :]).then_inc(s["stored"], 16)
            sp.wait_ge(s["stored"], 16 * (NCH + 1))

        @block.gpsimd
        def _(pool):
            pool.memset(ident[:, :], 0.0).then_inc(s["ident_cleared"], 1)
            pool.wait_ge(s["ident_cleared"], 1)
            pool.affine_select(out=ident[:, :], in_=ident[:, :], compare_op=ALU.not_equal, fill=1.0, base=0,
                               pattern=[[-1, P]], channel_multiplier=1).then_inc(s["ident_made"], 1)
            pool.wait_ge(s["ident_made"], 1)
            pool.tensor_copy(ident_b[:, :], ident[:, :]).then_inc(s["ident_made"], 1)
            for n in range(2):
                pool.memset(k_buf[n][:, :, :].bitcast(F32), 0.0).then_inc(s["fills_made"], 1)
            pool.memset(one_rows[:, :, :], 1.0).then_inc(s["fills_made"], 1)
            for n in range(SLOTS):
                pool.memset(q_buf[n][:, :, :].bitcast(F32), 0.0).then_inc(s["q_cleared"], 1)
            pool.memset(v_all[:, :, :, :, HD:VC], 1.0).then_inc(s["v_ones"], 1)
            pool.memset(zero_rows[:, :, :], 0.0).then_inc(s["q_cleared"], 1)
            pool.memset(ones[:, :], 1.0).then_inc(s["ones_made"], 1)
            pool.memset(zeros[:, :, :], 0.0).then_inc(s["ones_made"], 1)
            pool.wait_ge(s["ones_made"], 2)

            def residual2(n):
                chunk, is_k, _ = PROJ[n]
                pool.wait_ge(s["proj_copied"], n - NP0 + 1)
                pool.wait_ge(s["part_high"], n + 1)
                pool.tensor_tensor(resid[:, n % 4, :], resid[:, n % 4, :], split[:, chunk, is_k, 0, :],
                                   ALU.subtract).then_inc(s["resid_made2"], 1)

            def low2(n):
                chunk, is_k, _ = PROJ[n]
                pool.wait_ge(s["part_mid"], n + 1)
                pool.tensor_tensor(split[:, chunk, is_k, 2, :], resid[:, n % 4, :], split[:, chunk, is_k, 1, :],
                                   ALU.subtract).then_inc(s["part_low2"], 1)

            def split_max(v_next, pair):
                pool.wait_ge(s["max_done"], 2 + MT * (v_next - 1) + (pair + 1) * MT // 2)
                pool.tensor_tensor(mparts[:, pair, :, 0, :], negmax[:, pair, :, :], zeros[:, :, :],
                                   ALU.add).then_inc(s["max_split"], 1)
                pool.wait_ge(s["max_split"], 4 * v_next - 3 + 2 * pair)
                pool.tensor_tensor(mparts[:, pair, :, 1, :], negmax[:, pair, :, :], mparts[:, pair, :, 0, :],
                                   ALU.subtract).then_inc(s["max_split"], 1)

            def step(i, q):
                if start_of(i, q, LEAD_MA):
                    split_max(stream(i, q, LEAD_MA)[0] + 1, 0)
                if start_of(i, q, LEAD_MB):
                    split_max(stream(i, q, LEAD_MB)[0] + 1, 1)
                piece, n = PIECES.get(q - 2, (None, 0))
                if piece == "proj":
                    low2(n)
                piece, n = PIECES.get(q - 1, (None, 0))
                if piece == "proj":
                    residual2(n)
                if q == -1:
                    pool.wait_ge(s["gbb_tok_made"], 1)
                    pool.wait_ge(s["xn_made"], NT)
                    for n in range(CT, NT):
                        pool.tensor_tensor(x_sb[:, n, :], x_sb[:, n, :], gbb_tok[:, n // TB, :], ALU.add).then_inc(s["x_biased"], 1)

            pipeline(pool, step)

        @block.scalar
        def _(ac):
            ac.dma_start(c_sb[:, :], c).then_inc(s["c_in"], 16)
            for n, w in enumerate((w_q, w_k, w_v)):
                ac.dma_start(w_nat[:, n, :], w).then_inc(s["wts_in"], 16)
            ac.wait_ge(s["c_turned"], 1)
            ac.activation(c_t[:, 0, :], ps[:, 0, 384:384 + B], ACT.Exp, scale=-1.0).then_inc(s["silu"], 1)
            ac.wait_ge(s["w_turned"], 1)
            ac.activation(w_t[:, :, :], ps[:, 7, 0:384].rearrange("p (n d) -> p n d", n=3), ACT.Copy).then_inc(s["w_turned_sb"], 1)

            def modulate(n):
                b = n // HALVES
                ac.wait_ge(s["xn_turned"], n + 1)
                ac.activation(h_t[:, n * CH:(n + 1) * CH], ps[:, T_BANK[n], :], ACT.Identity,
                              bias=mod[:, 0, b:b + 1], scale=mod[:, 1, b:b + 1]).then_inc(s["h_made"], 1)

            def high(n):
                chunk, is_k, bank = PROJ[n]
                ac.wait_ge(s["qk_mm"], n + 1)
                ac.activation(split[:, chunk, is_k, 0, :], ps[:, bank, :], ACT.Copy).then_inc(s["part_high"], 1)

            def mid(n):
                chunk, is_k, _ = PROJ[n]
                if n < NP0:
                    ac.wait_ge(s["resid_made"], n + 1)
                else:
                    ac.wait_ge(s["resid_made2"], n - NP0 + 1)
                ac.activation(split[:, chunk, is_k, 1, :], resid[:, n % 4, :], ACT.Copy).then_inc(s["part_mid"], 1)

            def values(n):
                ac.wait_ge(s["v_ones"], 1)
                ac.wait_ge(s["v_mm"], n + 1)
                for t in range(CT):
                    tile = n * CT + t
                    ac.activation(v_all[:, (tile // TB) * (G // B):(tile // TB + 1) * (G // B), tile % TB, :, 0:HD],
                                  ps[:, V_BANK[n], t * P:(t + 1) * P].rearrange("p (q j d) -> p q j d", q=G // B, j=QH),
                                  ACT.Copy).then_inc(s["v_made"], 1)

            ac.wait_ge(s["mod_made"], 2)
            modulate(0)
            modulate(1)
            high(0)
            for n in range(NP0):
                if n + 1 < NP0:
                    high(n + 1)
                mid(n)
            values(0)
            values(1)
            modulate(2)

            def copy_max(pair, v_next):
                ac.wait_ge(s["m_turned"], 2 * v_next - 1 + pair)
                ac.activation(mrow_sb[pair][:, :], misc_b[0:2 * MROWS * CT, 0:P], ACT.Copy).then_inc(s["m_copied"], 1)

            def copy_acc(u_next):
                ac.wait_ge(s["value_mm"], PRING + KT * u_next)
                ac.wait_ge(s["acc_copied_v"], u_next)
                ac.activation(o_sb[:, 0:CH // 2], acc[:, 0:CH // 2], ACT.Copy).then_inc(s["acc_copied"], 1)

            misc_b = misc.bitcast(BF16)[:, 0:CH]

            def step(i, q):
                now = stream(i, q, LEAD_COL)
                for j in range(QH):
                    if now:
                        u, _, kt = now
                        if j == 0:
                            ac.wait_ge(s["value_mm"], KT * u + kt + 1)
                        ac.wait_ge(s["col_mm"], XB * u + kt * QH + j + 1)
                        ac.activation(probs[:, kt % PRING, j, :], ps[:, col_bank(i, q, j), :], ACT.Exp,
                                      scale=SCALE).then_inc(s["exp_done"], 1)
                    if j == 1 and start_of(i, q - 1, LEAD_MA):
                        copy_max(0, stream(i, q - 1, LEAD_MA)[0] + 1)
                    if j == 1 and start_of(i, q - 1, LEAD_MB):
                        copy_max(1, stream(i, q - 1, LEAD_MB)[0] + 1)
                    if j == 3 and start_of(i, q, LEAD_ACC):
                        copy_acc(stream(i, q, LEAD_ACC)[0] + 1)
                piece, n = PIECES.get(q, (None, 0))
                if piece == "turn":
                    modulate(n)
                if piece == "proj":
                    ac.wait_ge(s["qk_mm"], n + 1)
                    ac.wait_ge(s["part_low"], NP0)
                    ac.activation(resid[:, n % 4, :], ps[:, PROJ[n][2], :], ACT.Copy).then_inc(s["proj_copied"], 1)
                    high(n)
                piece, n = PIECES.get(q - 1, (None, 0))
                if piece == "proj":
                    mid(n)
                piece, n = PIECES.get(q, (None, 0))
                if piece == "values":
                    values(n)
                    values(n + 1)
                if piece == "clear":
                    ac.activation(credit[:, 1:2], ident[:, 0:1], ACT.Copy).then_inc(s["exp_done"], 2)
                if piece == "gates":
                    ac.wait_ge(s["gates_turned"], 1)
                    ac.activation(gbb_tok[:, :, :], misc[:, 0:B * D].rearrange("p (b d) -> p b d", b=B),
                                  ACT.Copy).then_inc(s["gbb_tok_made"], 1)
                    ac.activation(wo_t[:, :, :], misc[:, B * D:2 * B * D].rearrange("p (b d) -> p b d", b=B),
                                  ACT.Copy).then_inc(s["wo_turned_sb"], 1)

            pipeline(ac, step)

            def gelu(i, n):
                g = i * 2 * FB + n
                ac.wait_ge(s["ff1_mm"], g + 1)
                ac.wait_ge(s["gated"], g + 1)
                ac.activation(act[:, n % FRING, :], ff1_out[n % FRING], ACT.Gelu).then_inc(s["gelu_done"], 1)

            with ac.Fori(0, E // 2) as i:
                for n in range(2 * FB):
                    gelu(i, n)
            ac.wait_ge(s["ff2_mm"], E * FB)
            for n in range(2):
                half = slice(n * CH // 2, (n + 1) * CH // 2)
                ac.activation(y_t[:, half], ff2_out[:, half], ACT.Identity, bias=gbb[:, 0:1], scale=mod[:, 5, 0:1]).then_inc(s["y_sb"], 1)

        @block.vector
        def _(v):
            def rstd_chain(a, b, var_sem, count, done, base, between=None):
                v.wait_ge(var_sem, count)
                y, half_bits = rs[:, 3, a:b], rs[:, 2, a:b].bitcast(I32)
                v.tensor_scalar(half_bits, ve[:, a:b].bitcast(I32), 1, None, ALU.logical_shift_right).then_inc(done, 1)
                v.wait_ge(done, base + 1)
                v.tensor_scalar(y.bitcast(I32), half_bits, -1, RSQRT_BITS, ALU.mult, ALU.add).then_inc(done, 1)
                for n in range(3):
                    if between:
                        between(n)
                    v.wait_ge(done, base + 2 + 3 * n)
                    v.tensor_tensor(rs[:, 0, a:b], y, ve[:, a:b], ALU.mult).then_inc(done, 1)
                    v.wait_ge(done, base + 3 + 3 * n)
                    v.scalar_tensor_tensor(out=rs[:, 1, a:b], in0=rs[:, 0, a:b], scalar=-0.5, in1=y,
                                           op0=ALU.mult, op1=ALU.mult).then_inc(done, 1)
                    v.wait_ge(done, base + 4 + 3 * n)
                    v.scalar_tensor_tensor(out=y, in0=rs[:, 1, a:b], scalar=1.5, in1=y,
                                           op0=ALU.add, op1=ALU.mult).then_inc(done, 1)
                v.wait_ge(done, base + CHAIN)

            def statistics(b):
                for t in range(TB):
                    n = b * TB + t
                    if t % CT == 0:
                        v.wait_ge(x_in[n // CT], 16)
                    v.bn_stats(bn[:, n, :], x_sb[:, n, :]).then_inc(s["stats"], 1)
                for t in range(TB):
                    n = b * TB + t
                    v.wait_ge(s["stats"], 2 * TB * b + t + 1)
                    v.bn_aggr(mv[:, n, :], bn[:, n, :]).then_inc(s["stats"], 1)
                v.wait_ge(s["stats"], 2 * TB * (b + 1))
                v.tensor_scalar(ve[:, b * TB:(b + 1) * TB], mv[:, b * TB:(b + 1) * TB, 1], EPS, None, ALU.add).then_inc(s["var_ready"], 1)

            def deviation(b, between=None):
                rstd_chain(b * TB, (b + 1) * TB, s["var_ready"], b + 1, s["rstd"], CHAIN * b, between)

            def normalised(n):
                for t in range(n * CT, (n + 1) * CT):
                    v.tensor_scalar(xn[:, t, :], x_sb[:, t, :], mv[:, t, 0:1], rs[:, 3, t:t + 1],
                                    ALU.subtract, ALU.mult).then_inc(s["xn_made"], 1)

            def residual(n):
                chunk, is_k, bank = PROJ[n]
                v.wait_ge(s["part_high"], n + 1)
                v.tensor_tensor(resid[:, n % 4, :], ps[:, bank, :], split[:, chunk, is_k, 0, :],
                                ALU.subtract).then_inc(s["resid_made"], 1)

            statistics(0)

            def silu(n):
                if n == 0:
                    v.wait_ge(s["silu"], 1)
                    v.tensor_scalar(c_t[:, 1, :], c_t[:, 0, :], 1.0, None, ALU.add).then_inc(s["silu_dve"], 1)
                    return
                v.wait_ge(s["silu_dve"], n)
                if n == 1:
                    v.reciprocal(c_t[:, 2, :], c_t[:, 1, :]).then_inc(s["silu_dve"], 1)
                else:
                    v.tensor_tensor(c_t[:, 3, :], ps[:, 0, 384:384 + B], c_t[:, 2, :], ALU.mult).then_inc(s["silu_dve"], 1)

            deviation(0, silu)
            normalised(0)
            def modulation(n, a, b, one):
                v.wait_ge(s["mod_mm"], n + 1)
                v.tensor_copy(mod[:, a:b, :], ps[:, 1, a * B:b * B].rearrange("p (n b) -> p n b", b=B)).then_inc(s["mod_made"], 1)
                v.wait_ge(s["mod_made"], 2 * n + 1)
                v.tensor_scalar(mod[:, one, :], mod[:, one, :], 1.0, None, ALU.add).then_inc(s["mod_made"], 1)

            modulation(0, 0, 2, 1)
            normalised(1)
            statistics(1)

            def low(n):
                chunk, is_k, _ = PROJ[n]
                v.wait_ge(s["part_mid"], n + 1)
                v.tensor_tensor(split[:, chunk, is_k, 2, :], resid[:, n % 4, :], split[:, chunk, is_k, 1, :],
                                ALU.subtract).then_inc(s["part_low"], 1)

            residual(0)
            for n in range(NP0 - 1):
                if n + 1 < NP0 - 1:
                    residual(n + 1)
                low(n)
            residual(NP0 - 1)
            low(NP0 - 1)
            modulation(1, 2, 6, 4)
            v.memset(credit[:, 0:1], 0.0).then_inc(s["max_done"], 2)
            deviation(1)
            normalised(2)
            normalised(3)
            def prepare(n):
                if n == 0:
                    v.wait_ge(s["mod_made"], 4)
                    v.tensor_scalar(sgn[:, :, :], mod[:, 2:6:3, :], 0.0, 2.0, ALU.is_ge, ALU.mult).then_inc(s["gates_made"], 1)
                    v.scalar_tensor_tensor(out=mag[:, :, :], in0=mod[:, 2:6:3, :], scalar=-1.0, in1=mod[:, 2:6:3, :],
                                           op0=ALU.mult, op1=ALU.max).then_inc(s["gates_made"], 1)
                if n == 1:
                    v.wait_ge(s["gates_made"], 2)
                    v.tensor_scalar(mag[:, :, :], mag[:, :, :], 0.25, None, ALU.max).then_inc(s["gates_made"], 1)
                    v.wait_ge(s["gates_made"], 3)
                    v.scalar_tensor_tensor(out=mod[:, 2:6:3, :], in0=sgn[:, :, :], scalar=-1.0, in1=mag[:, :, :],
                                           op0=ALU.add, op1=ALU.mult).then_inc(s["gates_made"], 1)
                    v.wait_ge(s["small_in"], 48)
                    v.wait_ge(s["gates_made"], 4)
                    v.tensor_scalar(gbb[:, :], mod[:, 5, :], bias_sb[:, 0:1], None, ALU.mult).then_inc(s["gbb_made"], 1)
                if n == 2:
                    v.wait_ge(s["wo_in"], 16)
                    for b in range(B):
                        v.tensor_scalar(wo_g[:, b, :], w_nat[:, 3, :], mod[:, 2, b:b + 1], None, ALU.mult).then_inc(s["wo_made"], 1)
                if n == 3:
                    v.wait_ge(s["gbb_made"], 1)
                    v.wait_ge(s["ones_made"], 1)
                    for b in range(B):
                        v.tensor_scalar(gbb_w[:, b, :], ones[:, :], gbb[:, b:b + 1], None, ALU.mult).then_inc(s["gbb_made"], 1)
                    v.tensor_copy(idx_f[:, :, :], idx_i[:, :, :]).then_inc(s["gate_made"], 1)
                if n in (4, 5):
                    v.wait_ge(s["gate_made"], 1)
                    for e in range((n - 4) * E // 2, (n - 3) * E // 2):
                        v.scalar_tensor_tensor(out=hit[:, e, :, :], in0=idx_f[:, :, :], scalar=float(e), in1=ew[:, :, :],
                                               op0=ALU.is_equal, op1=ALU.mult).then_inc(s["gate_made"], 1)
                if n == 6:
                    v.wait_ge(s["gate_made"], 1 + E)
                    v.tensor_reduce(gate[:, :, :].rearrange("p t e -> p e t"), hit[:, :, :, :], AX.X, ALU.add).then_inc(s["gate_made"], 1)

            def row_max(v_next, m):
                v.wait_ge(s["row_mm"], MT * (v_next - 1) + m + 1)
                j, t = m // CT, m % CT
                v.tensor_reduce(negmax[:, j // 2, j % 2, t:t + 1], row_scores[m % 2].rearrange("p a k -> p (a k)"),
                                AX.X, ALU.max, negate=True).then_inc(s["max_done"], 1)

            def normalise(u_next, b, quad, half):
                o = misc.rearrange("p (t j w) -> p t j w", t=CT, j=QH)
                v.wait_ge(s["o_turned"], u_next)
                v.reciprocal(o_rec[:, :, :], o[:, :, :, HD]).then_inc(s["o_rec_made"], 1)
                v.wait_ge(s["o_rec_made"], u_next)
                v.tensor_tensor(heads[:, b, half, :, bass.ds(quad * QH * HD, QH * HD)].rearrange("p t (j d) -> p t j d", j=QH),
                                o[:, :, :, 0:HD],
                                o_rec[:, :, :].rearrange("p t (j o) -> p t j o", o=1).to_broadcast([P, CT, QH, HD]),
                                ALU.mult).then_inc(s["o_made"], 1)

            def copy_heads(n):
                v.wait_ge(s["hd_turned"], n + 1)
                v.tensor_copy(heads_t[:, n, :], ps[:, 2, :]).then_inc(s["hd_sb"], 1)

            def add_projection(n):
                v.wait_ge(s["proj_mm"], n + 1)
                if n == 1:
                    v.wait_ge(s["x_biased"], NT - CT)
                chunk = slice(n * CT, (n + 1) * CT)
                v.tensor_tensor(res[:, chunk, :], ps[:, 3, :].rearrange("p (t d) -> p t d", t=CT), x_sb[:, chunk, :],
                                ALU.add).then_inc(s["x1_made"], 1)

            def second_norm():
                v.wait_ge(s["x1_made"], 1)
                for t in range(CT):
                    v.bn_stats(bn[:, t, :], res[:, t, :]).then_inc(s["st2"], 1)
                for t in range(CT):
                    v.wait_ge(s["st2"], t + 1)
                    v.bn_aggr(mv[:, t, :], bn[:, t, :]).then_inc(s["st2"], 1)
                v.wait_ge(s["st2"], 2 * CT)
                v.tensor_scalar(ve[:, 0:CT], mv[:, 0:CT, 1], EPS, None, ALU.add).then_inc(s["var2"], 1)
                rstd_chain(0, CT, s["var2"], 1, s["rstd2"], 0)
                for t in range(CT):
                    v.tensor_scalar(xn[:, t, :], res[:, t, :], mv[:, t, 0:1], rs[:, 3, t:t + 1],
                                    ALU.subtract, ALU.mult).then_inc(s["xn2"], 1)

            def step(i, q):
                now = stream(i, q, LEAD_ROW)
                piece, n = PIECES.get(q - 1, (None, 0))
                if piece == "gate rows":
                    v.wait_ge(s["gate_turned"], 1)
                    v.tensor_copy(gate_t[:, :], misc[0:E, :]).then_inc(s["gate_t_sb"], 1)
                if q in PREPARE:
                    prepare(PREPARE[q])
                if piece == "clear":
                    v.wait_ge(s["v_made"], NT)
                    v.memset(acc, 0.0).then_inc(s["value_mm"], PRING)
                if start_of(i, q, LEAD_ACC):
                    u = stream(i, q, LEAD_ACC)[0]
                    v.wait_ge(s["value_mm"], PRING + KT * (u + 1))
                    v.tensor_copy(o_sb[:, CH // 2:CH], acc[:, CH // 2:CH]).then_inc(s["acc_copied_v"], 1)
                if now:
                    for m in range(2 * now[2], 2 * now[2] + 2):
                        row_max(now[0] + 1, m)
                if start_of(i, q, 0):
                    u, t, _ = stream(i, q, 0)
                    normalise(u + 1, i // 2, i % 2 * 2 + t // 2, t % 2)
                piece, n = tail_piece(i, q)
                if piece == "turn":
                    copy_heads(n)
                if piece == "norm":
                    v.wait_ge(s["xn2_turned"], 1)
                    v.tensor_scalar(h2_t[:, :], ps[:, 2, :], mod[:, 4, 0:1], mod[:, 3, 0:1], ALU.mult, ALU.add).then_inc(s["h2_made"], 1)
                if piece == "proj":
                    add_projection(n)
                if piece == "proj" and n == 1:
                    second_norm()
                if piece == "proj" and n == NCH - 2:
                    v.wait_ge(s["gate_b_in"], 16)
                    v.tensor_copy(credit[:, 2:3], ones[:, 0:1]).then_inc(s["gated"], FRING)

            pipeline(v, step)

            def gates(i, n):
                v.wait_ge(s["gelu_done"], i * 2 * FB + n + 1)
                v.tensor_tensor(acg[:, n % FRING, :], act[:, n % FRING, :], gate_b[:, i * 2 + n // FB, :], ALU.mult).then_inc(s["gated"], 1)

            for n in range(2 * FB):
                gates(0, n)
                if n == 0:
                    copy_heads(NCH - 1)
                if n == 1:
                    add_projection(NCH - 1)
            with v.Fori(1, E // 2) as i:
                for n in range(2 * FB):
                    gates(i, n)
            for n in range(2):
                half = slice(n * CT // 2, (n + 1) * CT // 2)
                v.wait_ge(s["y_turned"], n + 1)
                v.tensor_tensor(res[:, half, :], ps[:, 3 + n, 0:CH // 2].rearrange("p (t d) -> p t d", t=CT // 2), res[:, half, :],
                                ALU.add).then_inc(s["y_added"], 1)

        @block.tensor
        def _(pe):
            pe.wait_ge(s["ident_made"], 2)
            def keep_warm(count):
                for n in range(count):
                    pe.matmul(ps[:, 6, 0:P], ident_b[:, :], ident_b[:, :], start=True, stop=True)

            keep_warm(WARM)
            pe.wait_ge(s["c_in"], 16)
            pe.transpose(ps[:, 0, 384:384 + B], c_sb[:, :], ident[0:B, 0:B]).then_inc(s["c_turned"], 1)
            pe.wait_ge(s["wts_in"], 48)
            for n in range(3):
                mm = pe.transpose(ps[:, 7, n * P:(n + 1) * P], w_nat[:, n, :], ident[:, :])
            mm.then_inc(s["w_turned"], 1)
            keep_warm(4)
            pe.wait_ge(s["silu_dve"], 3)
            pe.wait_ge(s["wmod_in"], 16)

            def modulation(a, b):
                for n in range(a, b):
                    mm = pe.matmul(ps[:, 1, n * B:(n + 1) * B], wmod_sb[:, n * D:(n + 1) * D], c_t[:, 3, :], start=True, stop=True)
                mm.then_inc(s["mod_mm"], 1)

            def turn_xn(n):
                for t in range(CT):
                    pe.wait_ge(s["xn_made"], n * CT + t + 1)
                    mm = pe.transpose(ps[:, T_BANK[n], t * P:(t + 1) * P], xn[:, n * CT + t, :], ident[:, :])
                mm.then_inc(s["xn_turned"], 1)

            def project(n):
                chunk, is_k, bank = PROJ[n]
                pe.wait_ge(s["h_made"], chunk + 1)
                pe.matmul(ps[:, bank, :], w_t[:, is_k, :], h_t[:, chunk * CH:(chunk + 1) * CH],
                          start=True, stop=True).then_inc(s["qk_mm"], 1)

            def project_v(n):
                for t in range(CT):
                    mm = pe.matmul(ps[:, V_BANK[n], t * P:(t + 1) * P], h_t[:, (n * CT + t) * P:(n * CT + t + 1) * P], w_t[:, 2, :],
                                   start=True, stop=True)
                mm.then_inc(s["v_mm"], 1)

            modulation(0, 2)
            keep_warm(8)
            turn_xn(0)
            turn_xn(1)
            pe.wait_ge(s["w_turned_sb"], 1)
            for n in range(NP0):
                project(n)
            pe.wait_ge(s["mod_made"], 1)
            modulation(2, 6)
            project_v(0)
            pe.wait_ge(s["resid_made"], 1)
            project_v(1)
            pe.wait_ge(s["resid_made"], 4)
            turn_xn(2)

            misc_b = misc.bitcast(BF16)[:, 0:CH]

            def row_tile(i, q, m):
                u, buf, _ = stream(i, q, LEAD_ROW)
                j, t = m // CT, m % CT
                if m == 0:
                    loads = i + (q + LEAD_ROW) // STEPS + 1
                    pe.wait_ge(q_in[buf], 64 * loads - 32)
                    if q == -LEAD_ROW:
                        pe.wait_ge(s["k_filled"], 64)
                    if buf % 2 == 0:
                        pe.wait_ge(k_in[buf // 2], 32 * loads)
                pe.wait_ge(s["max_done"], MT * u + m + 1)
                for a in range(S // 512):
                    mm = pe.matmul(row_scores[m % 2][:, a, :], q_buf[buf][:, j // 2, t * P:(t + 1) * P],
                                   k_buf[buf // 2][:, j, a * 512:(a + 1) * 512], start=True, stop=True)
                mm.then_inc(s["row_mm"], 1)

            def col_tile(i, q, j):
                u, buf, kt = stream(i, q, LEAD_COL)
                if kt == 0 and j == 0:
                    pe.wait_ge(s["m_rows_a"], 32 * (u + 1))
                if kt == 0 and j == 2:
                    pe.wait_ge(s["m_rows_b"], 32 * (u + 1))
                if in_tail(i, q) and j == 2:
                    pe.wait_ge(s["max_done"], 2 + MT * U)
                pe.wait_ge(s["exp_done"], XB * u + kt * QH + j + (-1 if in_tail(i, q - 1) else 1))
                pe.matmul(ps[:, col_bank(i, q, j), :], k_buf[buf // 2][:, j, kt * P:(kt + 1) * P], q_buf[buf][:, j // 2, :],
                          start=True, stop=True).then_inc(s["col_mm"], 1)

            def turn_max(v_next, pair):
                pe.wait_ge(s["max_split"], 4 * v_next - 2 + 2 * pair)
                pe.transpose(misc_b[0:2 * MROWS * CT, 0:P], mparts[:, pair, :, :, :].rearrange("p j w t -> p (j w t)"),
                             ident_b[:, :]).then_inc(s["m_turned"], 1)

            def turn_out(u_next):
                pe.wait_ge(s["acc_copied"], u_next)
                for t in range(CT):
                    mm = pe.transpose(misc[:, t * P:(t + 1) * P], o_sb[:, t * P:(t + 1) * P], ident[:, :])
                mm.then_inc(s["o_turned"], 1)

            def value_tile(i, q):
                u, t, kt = stream(i, q, LEAD_VALUE)
                pe.wait_ge(s["exp_done"], 2 + XB * u + QH * (kt + 1))
                if kt == 0:
                    if t % 2 == 0:
                        pe.wait_ge(v_in[t // 2], 16 * (i + (q + LEAD_VALUE) // STEPS + 1))
                    if type(u) is not int or u > 0:
                        pe.wait_ge(s["acc_copied"], u)
                for j in range(QH):
                    mm = pe.matmul(acc[32 * j:32 * j + VC, :], v_st[:, t // 2, kt, j, :], probs[:, kt % PRING, j, :],
                                   start=(kt == 0), stop=(kt == KT - 1))
                mm.then_inc(s["value_mm"], 1)

            def turn_heads(n):
                b, half = n // HALVES, n % HALVES
                if n > 0:
                    pe.wait_ge(s["hd_sb"], n)
                if n == NCH - 1:
                    pe.wait_ge(s["h2_made"], 1)
                for t in range(CT):
                    mm = pe.transpose(ps[:, 2, t * P:(t + 1) * P], heads[:, b, half, t, :], ident[:, :])
                mm.then_inc(s["hd_turned"], 1)

            def project_heads(n):
                pe.wait_ge(s["hd_sb"], n + 1)
                if n > 0:
                    pe.wait_ge(s["x1_made"], n)
                for t in range(CT):
                    mm = pe.matmul(ps[:, 3, t * P:(t + 1) * P], heads_t[:, n, t * P:(t + 1) * P], wo_t[:, n // HALVES, :],
                                   start=True, stop=True)
                mm.then_inc(s["proj_mm"], 1)

            def ff1(i, n):
                if n % FB == 0:
                    pe.wait_ge(s[f"w1_in{n // FB}"], 16 * (i + 1))
                pe.matmul(ff1_out[n % FRING], w1_sb[n // FB][:, (n % FB) * P:(n % FB + 1) * P], h2_t[:, :],
                          start=True, stop=True).then_inc(s["ff1_mm"], 1)

            def ff2(i, n, start, stop):
                if n % FB == 0:
                    pe.wait_ge(s[f"w2_in{n // FB}"], 16 * (i + 1))
                pe.wait_ge(s["gated"], FRING + i * 2 * FB + n + 1)
                pe.matmul(ff2_out, w2_sb[n // FB][:, n % FB, :], acg[:, n % FRING, :], start=start, stop=stop,
                          skip_group_check=True).then_inc(s["ff2_mm"], 1)

            def step(i, q):
                col, row, value = stream(i, q, LEAD_COL), stream(i, q, LEAD_ROW), stream(i, q, LEAD_VALUE)
                if col:
                    col_tile(i, q, 0)
                    col_tile(i, q, 1)
                if value:
                    value_tile(i, q)
                if col:
                    col_tile(i, q, 2)
                    col_tile(i, q, 3)
                if row:
                    row_tile(i, q, 2 * row[2])
                    row_tile(i, q, 2 * row[2] + 1)
                if start_of(i, q, 0):
                    u = stream(i, q, 0)[0]
                    pe.wait_ge(s["m_copied"], 2 * u + 5 if type(u) is not int else min(2 * u + 5, 2 * U))
                    if type(u) is int and u > U - 2:
                        pe.wait_ge(s["o_made"], u)
                    turn_out(u + 1)
                if q == -1:
                    pe.wait_ge(s["gate_t_sb"], 1)
                if start_of(i, q, LEAD_MA):
                    u = stream(i, q, LEAD_MA)[0]
                    if type(u) is not int or u > 0:
                        pe.wait_ge(s["m_copied"], 2 * u)
                    turn_max(u + 1, 0)
                if start_of(i, q, LEAD_MB):
                    u = stream(i, q, LEAD_MB)[0]
                    pe.wait_ge(s["m_copied"], 2 * u + 1)
                    if type(u) is not int or u > 1:
                        pe.wait_ge(s["o_made"], u - 1)
                    turn_max(u + 1, 1)
                piece, n = PIECES.get(q, (None, 0))
                if piece == "turn":
                    turn_xn(n)
                if piece == "proj":
                    if n == 5:
                        pe.wait_ge(s["v_made"], 2 * CT)
                    elif n > 5:
                        pe.wait_ge(s["part_high"], n - 1)
                    project(n)
                if piece == "values":
                    pe.wait_ge(s["h_made"], n + 2)
                    project_v(n)
                    pe.wait_ge(s["part_high"], 7)
                    project_v(n + 1)
                if piece == "gates":
                    pe.wait_ge(s["m_copied"], 3)
                    pe.wait_ge(s["gbb_made"], 1 + B)
                    for b in range(B):
                        pe.matmul(misc[:, b * D:(b + 1) * D], gbb_w[:, b, :], ident[:, :], start=True, stop=True)
                    pe.wait_ge(s["wo_made"], B)
                    for b in range(B):
                        mm = pe.transpose(misc[:, (B + b) * D:(B + b + 1) * D], wo_g[:, b, :], ident[:, :])
                    mm.then_inc(s["gates_turned"], 1)
                if piece == "gate rows":
                    pe.wait_ge(s["wo_turned_sb"], 1)
                    pe.wait_ge(s["gate_made"], 2 + E)
                    for t in range(CT):
                        mm = pe.transpose(misc[0:E, t * P:(t + 1) * P], gate[:, t, :], ident[:, :])
                    mm.then_inc(s["gate_turned"], 1)
                piece, n = tail_piece(i, q)
                if piece == "turn":
                    pe.wait_ge(s["max_done"], 2 + MT * U)
                    pe.wait_ge(s["o_made"], min(U, (U // 2) * (n // HALVES + 1)) - (1 if n == NCH - 2 else 0))
                    turn_heads(n)
                if piece == "proj":
                    project_heads(n)
                if piece == "ff1":
                    pe.wait_ge(s["exp_done"], 2 + XB * U)
                    pe.wait_ge(s["h2_made"], 1)
                    ff1(0, 0)
                if piece == "norm":
                    pe.wait_ge(s["hd_sb"], 3)
                    for t in range(CT):
                        pe.wait_ge(s["xn2"], t + 1)
                        mm = pe.transpose(ps[:, 2, t * P:(t + 1) * P], xn[:, t, :], ident[:, :])
                    mm.then_inc(s["xn2_turned"], 1)
                if PIECES.get(q - 1, (None, 0))[0] == "clear":
                    pe.wait_ge(s["value_mm"], PRING)

            pipeline(pe, step)

            def experts(i, first, last):
                for n in range(2 * FB):
                    if n + AHEAD < 2 * FB:
                        ff1(i, n + AHEAD)
                    elif not last:
                        ff1(i + 1, n + AHEAD - 2 * FB)
                    ff2(i, n, first and n == 0, last and n == 2 * FB - 1)
                    if first and n == 0:
                        project_heads(NCH - 1)

            ff1(0, 1)
            pe.wait_ge(s["o_made"], U)
            turn_heads(NCH - 1)
            experts(0, True, False)
            with pe.Fori(1, E // 2 - 1) as i:
                experts(i, False, False)
            experts(E // 2 - 1, False, True)
            pe.wait_ge(s["x1_made"], NCH)
            for t in range(CT):
                half = t * 2 // CT
                pe.wait_ge(s["y_sb"], half + 1)
                mm = pe.transpose(ps[:, 3 + half, t % (CT // 2) * P:(t % (CT // 2) + 1) * P], y_t[:, t * P:(t + 1) * P], ident[:, :])
                if t % (CT // 2) == CT // 2 - 1:
                    mm.then_inc(s["y_turned"], 1)


LEAD_ACC = 2
LEAD_VALUE = 9
LEAD_COL = LEAD_VALUE + 2
LEAD_MB = LEAD_COL + 3
LEAD_MA = LEAD_MB + 3
LEAD_ROW = LEAD_MB + 8
LEAD_LOAD_V = 24
LEAD_LOAD = 27

_INS = ["L0_attn_x", "L0_attn_w_q", "L0_attn_w_k", "L0_attn_w_v", "L0_attn_w_o", "L0_ffn_expert_weights",
        "L0_ffn_expert_indices", "L0_ffn_w1", "L0_ffn_w2", "L0_ffn_bias", "L0_c", "L0_wmod"]


def kernel(**inputs):
    import numpy as _np
    import concourse.bacc as _bacc
    from concourse import mybir as _mybir
    from concourse.bass_utils import run_bass_kernel_spmd as _run

    nc = _bacc.Bacc("TRN2", target_bir_lowering=False, num_devices=1)
    arrays, args = {}, []
    for name in _INS:
        a = _np.ascontiguousarray(inputs[name])
        arrays[f"in_{name}_dram"] = a
        args.append(nc.dram_tensor(f"in_{name}_dram", a.shape, _mybir.dt.from_np(a.dtype), kind="ExternalInput").ap())
    out = nc.dram_tensor("out_dram", inputs["L0_attn_x"].shape, _mybir.dt.float32, kind="ExternalOutput").ap()
    adaln_block(nc, *args, out)
    r = _run(nc, [arrays], core_ids=[0])
    return r.results[0]["out_dram"]
```
